# Optimizing a Trainium2 kernel written in Bass

```python
import numpy as np
import jax
import jax.numpy as jnp

def _softmax(x, axis=-1):
    return jax.nn.softmax(x, axis=axis)

def _gelu(x):
    return jax.nn.gelu(x, approximate=True)

def _silu(x):
    return jax.nn.silu(x)

def _sigmoid(x):
    return jax.nn.sigmoid(x)

def _layernorm(x, axis=-1, eps=1e-05):
    m = jnp.mean(x, axis=axis, keepdims=True)
    v = jnp.var(x, axis=axis, keepdims=True)
    return (x - m) / jnp.sqrt(v + eps)

def _scatter_add(tgt, idx, src, axis=0):
    return tgt.at[idx].add(src)

def _segment_sum(src, seg, n):
    return jax.ops.segment_sum(src, seg, n)
kernel_name = 'mk_xattn_seq_d1_seqx_r4_006ec0'

def setup_inputs(seed: int=0):
    np.random.seed(seed)
    _w = jnp.asarray

    def _rec_inputs():
        import jax
        import jax.numpy as jnp
        _rk = jax.random.key(seed)
        x = -0.0002928 + 1 * jax.random.normal(jax.random.fold_in(_rk, 1), (16, 256, 256), jnp.float32)
        _lenS = 256 - jax.random.randint(jax.random.fold_in(_rk, 7), (16,), 0, max(1, 256 // 4) + 1, jnp.int32)
        _lenS2 = 77 - jax.random.randint(jax.random.fold_in(_rk, 8), (16,), 0, max(1, 77 // 4) + 1, jnp.int32)
        _ctx_1024P = jax.random.normal(jax.random.fold_in(_rk, 11), (16, 16, 256), jnp.float32)
        _ctx_1024c = jax.random.dirichlet(jax.random.fold_in(_rk, 511), 0.3 * jnp.ones((16,), jnp.float32), (16, 77))
        _ctx_1024t = jnp.einsum('bsk,bkd->bsd', _ctx_1024c, _ctx_1024P)
        _ctx_1024t = _ctx_1024t * jax.lax.rsqrt(jnp.mean(jnp.square(_ctx_1024t)) + 1e-12) * 0.953939
        ctx_1024 = -1.39393e-06 + 0.999914 * (_ctx_1024t + 0.3 * jax.random.normal(jax.random.fold_in(_rk, 611), (16, 77, 256), jnp.float32))
        return (x, ctx_1024)
    x, ctx_1024 = _rec_inputs()

    def _L0_xattn_setup():
        import jax, jax.numpy as jnp
        import numpy as np
        D_MODEL = 256
        N_HEADS = 16
        D_K = D_MODEL // N_HEADS
        LN_EPS = 1e-05

        def _attention(query, key_value, W_qkv, b_qkv, W_o, b_o, ln_gamma, ln_beta):
            B, Sq, _ = query.shape
            Skv = key_value.shape[1]
            Wq, Wk, Wv = (W_qkv[:D_MODEL], W_qkv[D_MODEL:2 * D_MODEL], W_qkv[2 * D_MODEL:])
            bq, bk, bv = (b_qkv[:D_MODEL], b_qkv[D_MODEL:2 * D_MODEL], b_qkv[2 * D_MODEL:])
            Q = (query @ Wq.T + bq).reshape(B, Sq, N_HEADS, D_K).transpose(0, 2, 1, 3)
            K = (key_value @ Wk.T + bk).reshape(B, Skv, N_HEADS, D_K).transpose(0, 2, 1, 3)
            V = (key_value @ Wv.T + bv).reshape(B, Skv, N_HEADS, D_K).transpose(0, 2, 1, 3)
            scores = jnp.einsum('bhqd,bhkd->bhqk', Q.astype(jnp.float32), K.astype(jnp.float32))
            scores = scores / np.sqrt(D_K)
            attn = jax.nn.softmax(scores, axis=-1)
            context = jnp.einsum('bhqk,bhkd->bhqd', attn, V.astype(jnp.float32)).astype(query.dtype)
            context = context.transpose(0, 2, 1, 3).reshape(B, Sq, D_MODEL)
            output = context @ W_o.T + b_o
            x = output + query
            mu = jnp.mean(x, axis=-1, keepdims=True)
            var = jnp.mean(jnp.square(x - mu), axis=-1, keepdims=True)
            return (x - mu) / jnp.sqrt(var + LN_EPS) * ln_gamma + ln_beta
        key = jax.random.key(seed)
        ks = jax.random.split(key, 8)
        B, Sq, Skv = (2, 512, 512)
        scale = 1.0 / np.sqrt(D_MODEL)
        return {'query': jax.random.normal(ks[0], (B, Sq, D_MODEL), dtype=jnp.float32), 'key_value': jax.random.normal(ks[1], (B, Skv, D_MODEL), dtype=jnp.float32), 'W_qkv': jax.random.normal(ks[2], (3 * D_MODEL, D_MODEL), dtype=jnp.float32) * scale, 'b_qkv': jax.random.normal(ks[3], (3 * D_MODEL,), dtype=jnp.float32) * 0.01, 'W_o': jax.random.normal(ks[4], (D_MODEL, D_MODEL), dtype=jnp.float32) * scale, 'b_o': jax.random.normal(ks[5], (D_MODEL,), dtype=jnp.float32) * 0.01, 'ln_gamma': jnp.ones((D_MODEL,), dtype=jnp.float32), 'ln_beta': jnp.zeros((D_MODEL,), dtype=jnp.float32)}
    _L0_xattn_all = _L0_xattn_setup()
    _L0_xattn_in = {k: v for k, v in _L0_xattn_all.items() if k in ('W_qkv', 'b_qkv', 'W_o', 'b_o', 'ln_gamma', 'ln_beta')}
    del _L0_xattn_all
    return {'x': x, 'ctx_1024': ctx_1024, 'L0_xattn_W_qkv': _L0_xattn_in['W_qkv'], 'L0_xattn_b_qkv': _L0_xattn_in['b_qkv'], 'L0_xattn_W_o': _L0_xattn_in['W_o'], 'L0_xattn_b_o': _L0_xattn_in['b_o'], 'L0_xattn_ln_gamma': _L0_xattn_in['ln_gamma'], 'L0_xattn_ln_beta': _L0_xattn_in['ln_beta']}

def reference(x, ctx_1024, L0_xattn_W_qkv, L0_xattn_b_qkv, L0_xattn_W_o, L0_xattn_b_o, L0_xattn_ln_gamma, L0_xattn_ln_beta):
    import jax
    import jax.numpy as jnp

    def _L0_xattn_ref(query, key_value, W_qkv, b_qkv, W_o, b_o, ln_gamma, ln_beta):
        import jax, jax.numpy as jnp
        import numpy as np
        D_MODEL = 256
        N_HEADS = 16
        D_K = D_MODEL // N_HEADS
        LN_EPS = 1e-05

        def _attention(query, key_value, W_qkv, b_qkv, W_o, b_o, ln_gamma, ln_beta):
            B, Sq, _ = query.shape
            Skv = key_value.shape[1]
            Wq, Wk, Wv = (W_qkv[:D_MODEL], W_qkv[D_MODEL:2 * D_MODEL], W_qkv[2 * D_MODEL:])
            bq, bk, bv = (b_qkv[:D_MODEL], b_qkv[D_MODEL:2 * D_MODEL], b_qkv[2 * D_MODEL:])
            Q = (query @ Wq.T + bq).reshape(B, Sq, N_HEADS, D_K).transpose(0, 2, 1, 3)
            K = (key_value @ Wk.T + bk).reshape(B, Skv, N_HEADS, D_K).transpose(0, 2, 1, 3)
            V = (key_value @ Wv.T + bv).reshape(B, Skv, N_HEADS, D_K).transpose(0, 2, 1, 3)
            scores = jnp.einsum('bhqd,bhkd->bhqk', Q.astype(jnp.float32), K.astype(jnp.float32))
            scores = scores / np.sqrt(D_K)
            attn = jax.nn.softmax(scores, axis=-1)
            context = jnp.einsum('bhqk,bhkd->bhqd', attn, V.astype(jnp.float32)).astype(query.dtype)
            context = context.transpose(0, 2, 1, 3).reshape(B, Sq, D_MODEL)
            output = context @ W_o.T + b_o
            x = output + query
            mu = jnp.mean(x, axis=-1, keepdims=True)
            var = jnp.mean(jnp.square(x - mu), axis=-1, keepdims=True)
            return (x - mu) / jnp.sqrt(var + LN_EPS) * ln_gamma + ln_beta
        return _attention(query, key_value, W_qkv, b_qkv, W_o, b_o, ln_gamma, ln_beta)
    x = _L0_xattn_ref(x, ctx_1024, L0_xattn_W_qkv, L0_xattn_b_qkv, L0_xattn_W_o, L0_xattn_b_o, L0_xattn_ln_gamma, L0_xattn_ln_beta)
    return x

_drawn_inputs = setup_inputs


def setup_inputs(seed=0):
    import zlib

    import numpy as np

    out = dict(_drawn_inputs(seed))
    spreads = {'L0_xattn_ln_gamma': (1.0, 0.2), 'L0_xattn_ln_beta': (0.0, 0.1)}
    factors = {'L0_xattn_b_qkv': 6.543, 'L0_xattn_b_o': 6.257}
    for name, (base, spread) in spreads.items():
        noise = np.random.default_rng([zlib.crc32(name.encode()), seed]).standard_normal(out[name].shape)
        drawn = base * np.exp(spread * noise) if base else spread * noise
        out[name] = jnp.asarray(drawn.astype(out[name].dtype))
    for name, factor in factors.items():
        out[name] = (out[name] * factor).astype(out[name].dtype)
    return out
```

```python
import math
from contextlib import ExitStack

import concourse.bass as bass
from concourse import mybir

F32 = mybir.dt.float32
F32R = mybir.dt.float32r
BF16 = mybir.dt.bfloat16
FP16 = mybir.dt.float16
I32 = mybir.dt.int32
U32 = mybir.dt.uint32
ALU = mybir.AluOpType
ACT = mybir.ActivationFunctionType
AX = mybir.AxisListType

B, SQ, D, SKV, H = 16, 256, 256, 77, 16
DK = D // H
P = 128
HALVES = 2
HH = H // HALVES
KC = D // P
QT = SQ // P
PAIR = 2 * SQ
PACKED = HH * SKV
TILES = -(-PACKED // P)
WIDE = TILES * P
UNITS = HALVES * TILES // 2
DMAX_HEADS = HH // 2
DMAX = QT * HALVES * 2
VW = DK + 1
VP = 3
GROUP = 4
GROUPS = B // GROUP
GK = GROUP * SKV
KSLOTS = 4
PSLOTS = 4
P32SLOTS = 2
MROWS = 32
LOW_TILES = 3
LN_EPS = 1e-5
SCALE = 1.0 / math.sqrt(DK)
EXP_SHIFT = 10 * math.log(2.0)
NEWTON = 3
LOOP_STEPS = 4
LOOPS = 2
LOOP_FIRST = 4
LAST_STEP = B + 2
CHAIN = 4 + 3 * NEWTON


def segments():
    out = []
    for t in range(TILES):
        for h in range(HH):
            a, b = max(P * t, SKV * h), min(P * (t + 1), SKV * (h + 1))
            if a < b:
                out.append((t, h, a - P * t, a - SKV * h, b - a, len(out)))
    return out


SEGMENTS = segments()
NSEG = len(SEGMENTS)


class Step:

    def __init__(self, first, i=None):
        self.first, self.i = first, i
        s = first
        self.scores = 0 <= s < B
        self.maxima = -1 <= s < B - 1
        self.output = 0 <= s - 1 < B
        self.norm = 0 <= s - 2 < B
        self.store = 0 <= s - 3 < B
        self.project_q = s % 2 == 0 and 0 <= s <= B - 4
        self.split_x = s % 2 == 1 and -1 <= s <= B - 5
        self.load_k = s % 2 == 0 and 2 <= s <= B - 4

    def lin(self, a, c, by=1):
        v = (a * self.first + c) // by
        return v if self.i is None else self.i * (a * LOOP_STEPS // by) + v

    def wait(self, eng, sem, a, c, by=1):
        if (a * self.first + c) // by > (0 if self.i is None else -1):
            eng.wait_ge(sem, self.lin(a, c, by))

    def batch(self, tensor, back, axis):
        if self.i is None:
            return tensor[self.first - back] if axis == 0 else tensor[:, self.first - back]
        at = bass.ds(self.lin(1, -back), 1)
        return (tensor[at].squeeze(0) if axis == 0 else tensor[:, at].squeeze(1))


def all_steps(eng, emit):
    for s in range(-1, LOOP_FIRST):
        emit(Step(s))
    with eng.Fori(0, LOOPS) as i:
        for k in range(LOOP_STEPS):
            emit(Step(LOOP_FIRST + k, i))
    for s in range(LOOP_FIRST + LOOPS * LOOP_STEPS, LAST_STEP + 1):
        emit(Step(s))


def cross_attention_kernel(nc, xT, x, cT, wqT, wkT, wvT, woT, bq, bk, bv, bo, gamma, beta, ident,
                           minus_low, minus_high, out):
    ctx = ExitStack()
    with ctx:
        def sb(name, shape, dt, stack=ctx):
            return stack.enter_context(nc.sbuf_tensor(name, shape, dt))

        def sem(name):
            return ctx.enter_context(nc.semaphore(name))

        wq_h, wq_l = sb("wq_h", [P, KC, D], F32R), sb("wq_l", [P, KC, D], F32R)
        wo_h, wo_l = sb("wo_h", [P, KC, D], F32R), sb("wo_l", [P, KC, D], F32R)
        kT = sb("kT", [P, B, HALVES, 2, SKV], F32R)
        kblk = sb("kblk", [P, KSLOTS, HALVES, 2, WIDE], F32R)
        vparts = sb("vparts", [SKV, B, H, VP, VW], BF16)
        vblk_all = sb("vblk", [P, B * HALVES * NSEG * VP * VW], BF16)
        vblk = vblk_all[:].rearrange("p (b f n v w) -> p b f n v w", f=HALVES, n=NSEG, v=VP, w=VW)
        xT_raw = sb("xT_raw", [P, KC, PAIR], F32)
        xT_h, xT_l = sb("xT_h", [P, KC, PAIR], F32R), sb("xT_l", [P, KC, PAIR], F32R)
        q_low = [sb(f"q_low{n}", [P, HALVES, PAIR], F32R) for n in range(2)]
        q_high = [sb(f"q_high{n}", [P, HALVES, PAIR], F32R) for n in range(2)]
        q_lo = [sb(f"q_lo{n}", [P, HALVES, PAIR], F32R) for n in range(2)]
        ident_sb = sb("ident_sb", [P, P], F32)
        bq_sb, bk_sb, bv_sb = sb("bq_sb", [P, HALVES], F32), sb("bk_sb", [P, HALVES], F32), sb("bv_sb", [P, KC], F32)
        bo_sb = sb("bo_sb", [P, D], F32)
        gamma_sb, beta_sb = sb("gamma_sb", [P, D], F32), sb("beta_sb", [P, D], F32)
        maxima = sb("maxima", [P, QT, MROWS], F32)
        shift = sb("shift", [P, 1], F32)
        recip = sb("recip", [P, QT, H], F32)
        stats = sb("stats", [P, QT, 6], F32)
        meanvar = sb("meanvar", [P, QT, 2], F32)
        rs_v, rs_y, rs_t = sb("rs_v", [P, QT], F32), sb("rs_y", [P, QT], F32), sb("rs_t", [P, QT], F32)

        early = ExitStack()
        w_raw = sb("w_raw", [P, 4, KC, D], F32, early)
        wk_h, wk_l = sb("wk_h", [P, KC, D], F32R, early), sb("wk_l", [P, KC, D], F32R, early)
        wv_h, wv_l = sb("wv_h", [P, KC, D], F32R, early), sb("wv_l", [P, KC, D], F32R, early)
        c_raw = sb("c_raw", [P, 2, KC, GK], F32, early)
        c_h, c_l = sb("c_h", [P, 2, KC, GK], F32R, early), sb("c_l", [P, 2, KC, GK], F32R, early)
        vrest = sb("vrest", [SKV, 2, 2, D], F32, early)
        early.close()
        p32 = sb("p32", [P, P32SLOTS, 2, SQ], F32)
        p_h, p_l = sb("p_h", [P, PSLOTS, 2, SQ], FP16), sb("p_l", [P, PSLOTS, 2, SQ], FP16)
        ctx_n = sb("ctx_n", [P, QT, D], F32)
        ctx_h, ctx_l = sb("ctx_h", [P, HALVES, SQ], F32R), sb("ctx_l", [P, HALVES, SQ], F32R)
        y = sb("y", [P, QT, D], F32)
        x_rows = sb("x_rows", [P, 2, QT, D], F32)
        result = sb("result", [P, 2, QT, D], F32)

        def bank(name, shape):
            return ctx.enter_context(nc.psum_tensor(name, shape, F32))

        ps_s = [bank(f"ps_s{n}", [P, 2, SQ]) for n in range(2)]
        ps_acc = [bank(f"ps_acc{n}", [P, 512]) for n in range(2)]
        ps_d = [bank(f"ps_d{n}", [P, 512]) for n in range(2)]
        ps_x = [bank(f"ps_x{n}", [P, 512]) for n in range(2)]

        ld_w = [sem(f"ld_w{n}") for n in range(4)]
        ld_c = [sem(f"ld_c{n}") for n in range(2)]
        ld_const, ld_minus = sem("ld_const"), sem("ld_minus")
        ld_xT = sem("ld_xT")
        ld_k = [sem(f"ld_k{n}") for n in range(2)]
        ld_v = sem("ld_v")
        ld_x = [sem(f"ld_x{n}") for n in range(2)]
        st_out = [sem(f"st_out{n}") for n in range(2)]
        cleared_k, cleared_v, cleared_parts, cleared_m = sem("cleared_k"), sem("cleared_v"), sem("cleared_parts"), sem("cleared_m")
        minus_set, shift_set = sem("minus_set"), sem("shift_set")
        w_hi, w_lo = sem("w_hi"), sem("w_lo")
        c_hi, c_lo = sem("c_hi"), sem("c_lo")
        bo_done = sem("bo_done")
        pe_bo, pe_k, pe_v = sem("pe_bo"), sem("pe_k"), sem("pe_v")
        k_hi, k_lo = sem("k_hi"), sem("k_lo")
        v_hi, v_rest1, v_mid, v_low = sem("v_hi"), sem("v_rest1"), sem("v_mid"), sem("v_low")
        x_hi, x_lo = sem("x_hi"), sem("x_lo")
        pe_q, q_hi, q_lo_done = sem("pe_q"), sem("q_hi"), sem("q_lo_done")
        pe_d, max_done, pe_m, m_done = sem("pe_d"), sem("max_done"), sem("pe_m"), sem("m_done")
        pe_s, exp32, exp16, rest16 = sem("pe_s"), sem("exp32"), sem("exp16"), sem("rest16")
        pe_e, rec_done, norm_done = sem("pe_e"), sem("rec_done"), sem("norm_done")
        pe_t, ctx_hi, ctx_lo = sem("pe_t"), sem("ctx_hi"), sem("ctx_lo")
        pe_o, x_biased, y_done = sem("pe_o"), sem("x_biased"), sem("y_done")
        stats_done, var_done, newton, centred, scaled, result_done = (
            sem("stats_done"), sem("var_done"), sem("newton"), sem("centred"), sem("scaled"), sem("result_done"))

        block = ctx.enter_context(nc.Block())

        xT_v = xT.rearrange("(k p) q -> p k q", p=P)
        cT_v = cT.rearrange("(k p) q -> p k q", p=P)
        x_v = x.rearrange("(b t p) d -> b p t d", p=P, t=QT)
        out_v = out.rearrange("(b t p) d -> b p t d", p=P, t=QT)
        WK, WV, WQ, WO = range(4)
        split_w = {WK: (wk_h, wk_l), WQ: (wq_h, wq_l), WV: (wv_h, wv_l), WO: (wo_h, wo_l)}
        V_TASKS = B // 2
        low_rows, high_rows = slice(P - MROWS, P), slice(0, MROWS)
        low_cols, high_cols = LOW_TILES * P, PACKED - LOW_TILES * P
        v_batch = HALVES * NSEG * VP * VW
        stage = vblk_all[:, (B - 2) * v_batch:].bitcast(F32)
        stage_low = stage[low_rows, 0:HALVES * low_cols].rearrange("p (f c) -> p f c", f=HALVES)
        stage_high = stage[high_rows, 0:HALVES * high_cols].rearrange("p (f c) -> p f c", f=HALVES)
        CONSTS = 7

        @block.sync
        def _(sp):
            def load_weight(n, w):
                sp.dma_start(w_raw[:, n], w.rearrange("(k p) n -> p k n", p=P)).then_inc(ld_w[n], 16)

            def load_context(g):
                sp.dma_start(c_raw[:, g % 2], cT_v[:, :, g * GK:(g + 1) * GK]).then_inc(ld_c[g % 2], 16)

            def load_k(batch, slot):
                for h in range(HH):
                    rows = slice(DK * h, DK * (h + 1))
                    sp.dma_start(
                        kblk[rows, 2 * slot:2 * slot + 2, :, :, SKV * h:SKV * (h + 1)].rearrange("p b f l k -> p (b f l) k").bitcast(F32),
                        kT[rows, bass.ds(batch, 2)].rearrange("p b f l k -> p (b f l) k").bitcast(F32)).then_inc(ld_k[slot], 16)

            load_weight(WK, wkT)
            load_context(0)
            load_weight(WQ, wqT)
            sp.dma_start(xT_raw[:], xT_v[:, :, 0:PAIR]).then_inc(ld_xT, 16)
            load_weight(WV, wvT)
            load_context(1)
            load_weight(WO, woT)
            for g in range(2, GROUPS):
                sp.wait_ge(c_hi, g - 1)
                sp.wait_ge(c_lo, g - 1)
                load_context(g)
            sp.wait_ge(cleared_k, 1)
            for pair in range(2):
                sp.wait_ge(k_hi, HALVES)
                sp.wait_ge(k_lo, HALVES)
                load_k(2 * pair, pair)

            def load_v():
                sp.wait_ge(cleared_v, 2)
                sp.wait_ge(cleared_parts, 2)
                sp.wait_ge(v_hi, V_TASKS)
                sp.wait_ge(v_mid, V_TASKS)
                sp.wait_ge(v_low, V_TASKS)
                src = vparts[:].rearrange("p b (f h) v w -> p (b f) h (v w)", h=HH)
                dst = vblk.rearrange("p b f n v w -> p (b f) n (v w)")
                for t, h, row, key, n, seg in SEGMENTS:
                    sp.dma_start(dst[row:row + n, :, seg], src[key:key + n, :, h]).then_inc(ld_v, 16)

            def step(S):
                s = S.first
                if S.split_x:
                    S.wait(sp, x_hi, 1, 3, by=2)
                    S.wait(sp, x_lo, 1, 3, by=2)
                    sp.dma_start(xT_raw[:], xT_v[:, :, bass.ds(S.lin(SQ, 3 * SQ), PAIR)]).then_inc(ld_xT, 16)
                if s == -1:
                    load_v()
                if S.load_k:
                    if s == 2:
                        sp.wait_ge(k_hi, HALVES * GROUPS)
                        sp.wait_ge(k_lo, HALVES * GROUPS)
                    S.wait(sp, pe_s, UNITS, 0)
                    load_k(S.lin(1, 2), (s // 2 + 1) % 2)
                if S.scores:
                    if s == 0:
                        sp.wait_ge(pe_v, V_TASKS)
                        sp.wait_ge(pe_bo, 1)
                    S.wait(sp, y_done, 1, -1)
                    sp.dma_start(x_rows[:, s % 2], S.batch(x_v, 0, 0)).then_inc(ld_x[s % 2], 16)
                if S.store:
                    S.wait(sp, result_done, 1, -2)
                    sp.dma_start(S.batch(out_v, 3, 0), result[:, (s - 3) % 2]).then_inc(st_out[(s - 3) % 2], 16)

            all_steps(sp, step)
            for n in range(2):
                sp.wait_ge(st_out[n], 16 * B // 2)

        @block.tensor
        def _(pe):
            def mm(o, w, m, start, stop):
                return nc.tensor.matmul(o, w, m, start=start, stop=stop, skip_group_check=True)

            def three(o, w, m):
                terms = [(a, b, k) for k in range(KC) for a, b in ((0, 0), (0, 1), (1, 0))]
                for n, (a, b, k) in enumerate(terms):
                    ins = mm(o, w(a, k), m(b, k), n == 0, n == len(terms) - 1)
                return ins

            def project_k(g):
                pe.wait_ge(c_hi, g + 1)
                pe.wait_ge(c_lo, g + 1)
                for f in range(HALVES):
                    if g:
                        pe.wait_ge(k_hi, HALVES * (g - 1) + f + 1)
                        pe.wait_ge(k_lo, HALVES * (g - 1) + f + 1)
                    three(ps_x[f][:, 0:GK], lambda a, k: (wk_h, wk_l)[a][:, k, f * P:(f + 1) * P],
                          lambda b, k: (c_h, c_l)[b][:, g % 2, k, :]).then_inc(pe_k, 1)

            def project_v(g):
                for n in range(2):
                    if g:
                        pe.wait_ge(v_hi, 2 * g + n - 1)
                        pe.wait_ge(v_rest1, 2 * g + n - 1)
                    for j in range(2):
                        at = (2 * n + j) * SKV
                        ins = three(ps_acc[n][0:SKV, j * D:(j + 1) * D],
                                    lambda a, k: (c_h, c_l)[a][:, g % 2, k, at:at + SKV],
                                    lambda b, k: (wv_h, wv_l)[b][:, k, :])
                    ins.then_inc(pe_v, 1)

            def project_q(f):
                three(ps_x[f][:], lambda a, k: (wq_h, wq_l)[a][:, k, f * P:(f + 1) * P],
                      lambda b, k: (xT_h, xT_l)[b][:, k, :]).then_inc(pe_q, 1)

            pe.wait_ge(w_hi, 1)
            pe.wait_ge(w_lo, 1)
            project_k(0)
            pe.wait_ge(w_hi, 2)
            pe.wait_ge(w_lo, 2)
            pe.wait_ge(x_hi, 1)
            pe.wait_ge(x_lo, 1)
            for f in range(HALVES):
                pe.wait_ge(k_hi, f + 1)
                pe.wait_ge(k_lo, f + 1)
                project_q(f)
            pe.wait_ge(w_hi, 3)
            pe.wait_ge(w_lo, 3)
            project_v(0)
            pe.wait_ge(q_hi, HALVES)
            pe.wait_ge(q_lo_done, HALVES)
            for g in range(1, GROUPS):
                project_k(g)
                project_v(g)
            pe.wait_ge(ld_const, 16 * CONSTS)
            pe.wait_ge(ld_w[WO], 16)
            pe.wait_ge(k_hi, HALVES * GROUPS)
            pe.wait_ge(k_lo, HALVES * GROUPS)
            for k in range(KC):
                ins = mm(ps_x[0][:, 0:D], bv_sb[:, k:k + 1].to_broadcast([P, P]), w_raw[:, WO, k, :], k == 0, k == KC - 1)
            ins.then_inc(pe_bo, 1)

            def step(S):
                s = S.first
                nb = s + 1

                def max_bank(j):
                    return ps_d[((DMAX + 1) * nb + j) % 2]

                def max_scores(j):
                    t, f, n = j // 4, j // 2 % 2, j % 2
                    if j == 0:
                        if nb % 2 == 0:
                            S.wait(pe, ld_k[nb // 2 % 2], 16 * HH, 16 * HH * (5 - nb % 4), by=4)
                            S.wait(pe, q_hi, 1, 3)
                        S.wait(pe, max_done, DMAX, DMAX)
                    elif j == 1:
                        S.wait(pe, m_done, 1, 1)
                    else:
                        S.wait(pe, max_done, DMAX, DMAX + j - 1)
                    q0 = nb % 2 * SQ + t * P
                    mm(max_bank(j)[:, 0:DMAX_HEADS * SKV], q_low[nb // 2 % 2][:, f, q0:q0 + P],
                       kblk[:, nb % KSLOTS, f, 0, n * DMAX_HEADS * SKV:(n + 1) * DMAX_HEADS * SKV],
                       True, True).then_inc(pe_d, 1)

                def turn_maxima():
                    S.wait(pe, max_done, DMAX, 2 * DMAX)
                    for t in range(QT):
                        ins = nc.tensor.transpose(max_bank(DMAX)[0:MROWS, t * P:(t + 1) * P], maxima[:, t, :], ident_sb[:])
                    ins.then_inc(pe_m, 1)

                def score_tile(u, n):
                    f, t = divmod(2 * u + n, TILES)
                    if n == 0:
                        S.wait(pe, exp16, UNITS, u - 1)
                    if u == 0 and n == 0:
                        S.wait(pe, m_done, 1, 1)
                        S.wait(pe, q_lo_done, 1, 2 - s % 2)
                        if s == 0:
                            pe.wait_ge(minus_set, 2)
                    tile = slice(t * P, (t + 1) * P)
                    cols = slice(s % 2 * SQ, (s % 2 + 1) * SQ)
                    q = (q_low if t < LOW_TILES else q_high)[s // 2 % 2][:, f, cols]
                    o = ps_s[(UNITS * s + u) % 2][:, n, :]
                    mm(o, kblk[:, s % KSLOTS, f, 0, tile], q, True, False)
                    mm(o, kblk[:, s % KSLOTS, f, 0, tile], q_lo[s // 2 % 2][:, f, cols], False, False)
                    ins = mm(o, kblk[:, s % KSLOTS, f, 1, tile], q, False, True)
                    if n == 1:
                        ins.then_inc(pe_s, 1)

                def weigh(u, n, back):
                    g = 2 * u + n
                    f, t = divmod(g, TILES)
                    slot = (UNITS * (s - back) + u) % PSLOTS
                    heads = [x[1] for x in SEGMENTS if x[0] == t]
                    s0 = [x[5] for x in SEGMENTS if x[0] == t][0]
                    h0 = f * HH + heads[0]
                    if n == 0:
                        S.wait(pe, exp16, UNITS, u + 1 - UNITS * back)
                        S.wait(pe, rest16, UNITS, u + 1 - UNITS * back)
                    if g == 0:
                        S.wait(pe, norm_done, QT, 0)
                        if s == 0:
                            pe.wait_ge(ld_v, 16 * NSEG)
                            pe.wait_ge(v_rest1, V_TASKS)
                    for qt in range(QT):
                        o = ps_acc[qt][:, h0 * VW:(h0 + len(heads)) * VW].rearrange("p (n w) -> p n w", w=VW)
                        for j, (p, v) in enumerate(((p_h, 0), (p_h, 1), (p_h, 2), (p_l, 0), (p_l, 1))):
                            ins = mm(o, p[:, slot, n, qt * P:(qt + 1) * P],
                                     S.batch(vblk, back, 1)[:, f, s0:s0 + len(heads), v, :],
                                     g == 0 and j == 0, g == HALVES * TILES - 1 and j == 4)
                    if n == 1:
                        ins.then_inc(pe_e, 1)

                def turn_context():
                    S.wait(pe, norm_done, QT, 0)
                    if S.project_q:
                        S.wait(pe, q_hi, 1, 3)
                        S.wait(pe, q_lo_done, 1, 3)
                    else:
                        S.wait(pe, ctx_hi, 1, -1)
                        S.wait(pe, ctx_lo, 1, -1)
                    for f in range(HALVES):
                        for qt in range(QT):
                            ins = nc.tensor.transpose(ps_x[0][:, f * SQ + qt * P:f * SQ + (qt + 1) * P],
                                                      ctx_n[:, qt, f * P:(f + 1) * P], ident_sb[:])
                    ins.then_inc(pe_t, 1)

                def project_out():
                    S.wait(pe, ctx_hi, 1, 0)
                    S.wait(pe, ctx_lo, 1, 0)
                    if S.project_q:
                        S.wait(pe, q_hi, 1, 4)
                        S.wait(pe, q_lo_done, 1, 4)
                    else:
                        S.wait(pe, y_done, 1, -1)
                    if s == 1:
                        pe.wait_ge(w_hi, 4)
                        pe.wait_ge(w_lo, 4)
                    for qt in range(QT):
                        ins = three(ps_x[1][:, qt * D:(qt + 1) * D],
                                    lambda a, k: (ctx_h, ctx_l)[a][:, k, qt * P:(qt + 1) * P],
                                    lambda b, k: (wo_h, wo_l)[b][:, k, :])
                    ins.then_inc(pe_o, 1)

                def next_q(f):
                    if f == 0:
                        S.wait(pe, x_hi, 1, 4, by=2)
                        S.wait(pe, x_lo, 1, 4, by=2)
                        S.wait(pe, ctx_hi, 1, -1)
                        S.wait(pe, ctx_lo, 1, -1)
                        if s == 0:
                            pe.wait_ge(bo_done, 1)
                    else:
                        S.wait(pe, y_done, 1, -1)
                    project_q(f)

                def next_maxima(j):
                    if S.maxima:
                        max_scores(j) if j < DMAX else turn_maxima()

                after_first, after_second, after_weigh = (0, 3, 6), (1, 4, 7), (2, 5)
                for u in range(UNITS):
                    if S.scores:
                        score_tile(u, 0)
                    if u < 3:
                        next_maxima(after_first[u])
                    if S.scores:
                        score_tile(u, 1)
                    if u < 3:
                        next_maxima(after_second[u])
                    for n in range(2):
                        if u < 2 and S.output:
                            weigh(u + 3, n, 1)
                        if u >= 2 and S.scores:
                            weigh(u - 2, n, 0)
                        if n == 0 and u < 2:
                            next_maxima(after_weigh[u])
                        if n == 0 and u == 3:
                            next_maxima(DMAX)
                    if u < 2 and S.project_q:
                        next_q(u)
                    if u == 2 and S.output:
                        turn_context()
                    if u == 4 and S.output:
                        project_out()

            all_steps(pe, step)

        @block.scalar
        def _(act):
            copy, add = ACT.Copy, ACT.Identity
            weights = list(split_w.items())

            for dst, src in ((ident_sb[:], ident), (bq_sb[:], bq), (bk_sb[:], bk), (bv_sb[:], bv),
                             (bo_sb[:], bo.partition_broadcast(P)), (gamma_sb[:], gamma.partition_broadcast(P)),
                             (beta_sb[:], beta.partition_broadcast(P))):
                act.dma_start(dst, src).then_inc(ld_const, 16)
            act.dma_start(stage_low, minus_low).then_inc(ld_minus, 16)
            act.dma_start(stage_high, minus_high).then_inc(ld_minus, 16)

            def weight_hi(n):
                w, (hi, _) = weights[n]
                act.wait_ge(ld_w[w], 16)
                nc.scalar.activation(hi[:], w_raw[:, w], copy).then_inc(w_hi, 1)

            def context_hi(g):
                act.wait_ge(ld_c[g % 2], 16 * (g // 2 + 1))
                if g >= 2:
                    act.wait_ge(pe_v, 2 * (g - 1))
                nc.scalar.activation(c_h[:, g % 2], c_raw[:, g % 2], copy).then_inc(c_hi, 1)

            def key_hi(g):
                for f in range(HALVES):
                    act.wait_ge(pe_k, HALVES * g + f + 1)
                    nc.scalar.activation(kT[:, GROUP * g:GROUP * (g + 1), f, 0, :],
                                         ps_x[f][:, 0:GK].rearrange("p (b k) -> p b k", k=SKV), add,
                                         bias=bk_sb[:, f:f + 1]).then_inc(k_hi, 1)

            def value_part(v, part):
                return vparts[:, 2 * v:2 * v + 2, :, part, 0:DK].rearrange("p b h w -> p (b h) w")

            def value_hi(v):
                act.wait_ge(pe_v, v + 1)
                nc.scalar.activation(value_part(v, 0), ps_acc[v % 2][0:SKV, :].rearrange("p (n w) -> p n w", w=DK),
                                     copy).then_inc(v_hi, 1)

            def value_mid(v):
                act.wait_ge(v_rest1, v + 1)
                nc.scalar.activation(value_part(v, 1), vrest[:, v % 2].rearrange("p b (h w) -> p (b h) w", w=DK),
                                     copy).then_inc(v_mid, 1)

            def query_hi(f, slot):
                nc.scalar.activation(q_low[slot][:, f], ps_x[f][:], add, bias=bq_sb[:, f:f + 1])
                nc.scalar.activation(q_high[slot][:, f], ps_x[f][:], add, bias=bq_sb[:, f:f + 1]).then_inc(q_hi, 1)

            weight_hi(0)
            context_hi(0)
            weight_hi(1)
            act.wait_ge(ld_xT, 16)
            nc.scalar.activation(xT_h[:], xT_raw[:], copy).then_inc(x_hi, 1)
            act.wait_ge(ld_const, 16 * CONSTS)
            key_hi(0)
            weight_hi(2)
            for f in range(HALVES):
                act.wait_ge(pe_q, f + 1)
                query_hi(f, 0)
            context_hi(1)
            value_hi(0)
            value_hi(1)
            value_mid(0)
            value_mid(1)
            for g in range(1, GROUPS):
                key_hi(g)
                if g + 1 < GROUPS:
                    context_hi(g + 1)
                value_hi(2 * g)
                value_hi(2 * g + 1)
                value_mid(2 * g)
                value_mid(2 * g + 1)
            weight_hi(3)

            def step(S):
                s = S.first

                def exponentials(u):
                    S.wait(act, pe_s, UNITS, u + 1)
                    S.wait(act, rest16, UNITS, u + 1 - P32SLOTS)
                    S.wait(act, pe_e, UNITS, u + 1 - PSLOTS)
                    if s == 0 and u == 0:
                        act.wait_ge(shift_set, 1)
                        act.wait_ge(pe_v, V_TASKS)
                        act.wait_ge(pe_bo, 1)
                        act.wait_ge(w_lo, 4)
                        act.wait_ge(v_low, V_TASKS)
                    n = UNITS * s + u
                    nc.scalar.activation(p32[:, n % P32SLOTS], ps_s[n % 2][:], ACT.Exp, bias=shift[:, 0:1],
                                         scale=SCALE).then_inc(exp32, 1)
                    nc.scalar.activation(p_h[:, n % PSLOTS], ps_s[n % 2][:], ACT.Exp, bias=shift[:, 0:1],
                                         scale=SCALE).then_inc(exp16, 1)

                for u in range(UNITS):
                    if S.scores:
                        exponentials(u)
                    if u < HALVES and S.project_q:
                        S.wait(act, pe_q, 1, 3 + u)
                        S.wait(act, pe_s, UNITS, 0)
                        query_hi(u, (s // 2 + 1) % 2)
                    if u == 2 and S.output:
                        S.wait(act, pe_t, 1, 0)
                        S.wait(act, pe_o, 1, -1)
                        nc.scalar.activation(ctx_h[:], ps_x[0][:].rearrange("p (f q) -> p f q", f=HALVES),
                                             copy).then_inc(ctx_hi, 1)
                    if u == 3 and S.maxima:
                        S.wait(act, pe_m, 1, 2)
                        nb = s + 1
                        cols = slice(nb % 2 * SQ, (nb % 2 + 1) * SQ)
                        m = ps_d[((DMAX + 1) * nb + DMAX) % 2][0:MROWS, 0:SQ].unsqueeze(1).broadcast_to([MROWS, HALVES, SQ])
                        nc.scalar.activation(q_low[nb // 2 % 2][low_rows, :, cols], m, copy)
                        nc.scalar.activation(q_high[nb // 2 % 2][high_rows, :, cols], m, copy).then_inc(m_done, 1)
                if S.split_x:
                    S.wait(act, ld_xT, 8, 8 * 5)
                    S.wait(act, pe_q, 1, 3)
                    nc.scalar.activation(xT_h[:], xT_raw[:], copy).then_inc(x_hi, 1)

            all_steps(act, step)

        @block.vector
        def _(dve):
            weights = list(split_w.items())
            v_ = nc.vector

            def lo(out_, whole, hi):
                return v_.tensor_tensor(out_, whole, hi.bitcast(F32), ALU.subtract)

            def lo_biased(out_, whole, bias, hi):
                return v_.scalar_tensor_tensor(out_, whole, bias, hi.bitcast(F32), ALU.add, ALU.subtract)

            v_.memset(maxima[:], 0.0).then_inc(cleared_m, 1)
            v_.memset(shift[:], EXP_SHIFT).then_inc(shift_set, 1)

            def weight_lo(n):
                w, (hi, low) = weights[n]
                dve.wait_ge(w_hi, n + 1)
                lo(low[:], w_raw[:, w], hi[:]).then_inc(w_lo, 1)

            def context_lo(g):
                dve.wait_ge(c_hi, g + 1)
                lo(c_l[:, g % 2], c_raw[:, g % 2], c_h[:, g % 2]).then_inc(c_lo, 1)

            def key_lo(g):
                for f in range(HALVES):
                    dve.wait_ge(k_hi, HALVES * g + f + 1)
                    part = kT[:, GROUP * g:GROUP * (g + 1), f]
                    lo_biased(part[:, :, 1, :], ps_x[f][:, 0:GK].rearrange("p (b k) -> p b k", k=SKV),
                              bk_sb[:, f:f + 1], part[:, :, 0, :]).then_inc(k_lo, 1)

            def value_part(v, part):
                return vparts[:, 2 * v:2 * v + 2, :, part, 0:DK].rearrange("p b h w -> p (b h) w")

            def value_rest(v):
                dve.wait_ge(v_hi, v + 1)
                if v >= 2:
                    dve.wait_ge(v_low, v - 1)
                v_.tensor_tensor(vrest[:, v % 2].rearrange("p b (h w) -> p (b h) w", w=DK),
                                 ps_acc[v % 2][0:SKV, :].rearrange("p (n w) -> p n w", w=DK),
                                 value_part(v, 0), ALU.subtract).then_inc(v_rest1, 1)

            def value_low(v):
                dve.wait_ge(v_mid, v + 1)
                v_.tensor_tensor(value_part(v, 2), vrest[:, v % 2].rearrange("p b (h w) -> p (b h) w", w=DK),
                                 value_part(v, 1), ALU.subtract).then_inc(v_low, 1)

            def query_lo(f, slot):
                lo_biased(q_lo[slot][:, f], ps_x[f][:], bq_sb[:, f:f + 1], q_high[slot][:, f]).then_inc(q_lo_done, 1)

            weight_lo(0)
            context_lo(0)
            weight_lo(1)
            dve.wait_ge(x_hi, 1)
            lo(xT_l[:], xT_raw[:], xT_h[:]).then_inc(x_lo, 1)
            dve.wait_ge(ld_const, 16 * CONSTS)
            key_lo(0)
            weight_lo(2)
            for f in range(HALVES):
                dve.wait_ge(q_hi, f + 1)
                query_lo(f, 0)
            context_lo(1)
            value_rest(0)
            value_rest(1)
            value_low(0)
            value_low(1)
            for g in range(1, GROUPS):
                key_lo(g)
                if g + 1 < GROUPS:
                    context_lo(g + 1)
                value_rest(2 * g)
                value_rest(2 * g + 1)
                value_low(2 * g)
                value_low(2 * g + 1)
            dve.wait_ge(cleared_k, 1)
            dve.wait_ge(ld_minus, 32)
            v_.tensor_copy(kblk[low_rows, :, :, 1, 0:low_cols].rearrange("p s f c -> p s f c"),
                           stage_low.unsqueeze(1).broadcast_to([MROWS, KSLOTS, HALVES, low_cols])).then_inc(minus_set, 1)
            v_.tensor_copy(kblk[high_rows, :, :, 1, low_cols:PACKED],
                           stage_high.unsqueeze(1).broadcast_to([MROWS, KSLOTS, HALVES, high_cols])).then_inc(minus_set, 1)
            weight_lo(3)
            dve.wait_ge(pe_bo, 1)
            v_.tensor_tensor(bo_sb[:], ps_x[0][:, 0:D], bo_sb[:], ALU.add).then_inc(bo_done, 1)
            dve.wait_ge(cleared_m, 1)

            def step(S):
                s = S.first

                def max_of(j):
                    t, f, n = j // 4, j // 2 % 2, j % 2
                    S.wait(dve, pe_d, DMAX, DMAX + j + 1)
                    if j == 0:
                        S.wait(dve, pe_m, 1, 1)
                    h0 = f * HH + n * DMAX_HEADS
                    v_.tensor_reduce(maxima[:, t, h0:h0 + DMAX_HEADS],
                                     ps_d[((DMAX + 1) * (s + 1) + j) % 2][:, 0:DMAX_HEADS * SKV]
                                     .rearrange("p (h k) -> p h k", k=SKV), AX.X, ALU.max).then_inc(max_done, 1)

                def normalize():
                    S.wait(dve, pe_e, UNITS, 0)
                    S.wait(dve, pe_t, 1, -1)
                    acc = [ps_acc[t][:, 0:H * VW].rearrange("p (h w) -> p h w", w=VW) for t in range(QT)]
                    for t in range(QT):
                        v_.reciprocal(recip[:, t], acc[t][:, :, DK]).then_inc(rec_done, 1)
                    for t in range(QT):
                        S.wait(dve, rec_done, QT, t + 1 - QT)
                        v_.tensor_tensor(ctx_n[:, t].rearrange("p (h w) -> p h w", w=DK), acc[t][:, :, 0:DK],
                                         recip[:, t].unsqueeze(2).broadcast_to([P, H, DK]), ALU.mult).then_inc(norm_done, 1)

                def layer_norm():
                    S.wait(dve, y_done, 1, -1)
                    done = [0]

                    def link(ins, needed=True):
                        done[0] += 1
                        ins.then_inc(newton, 1)
                        if needed:
                            S.wait(dve, newton, CHAIN, done[0] - 2 * CHAIN)

                    v_.bn_stats(stats[:, 0], y[:, 0]).then_inc(stats_done, 1)
                    S.wait(dve, stats_done, QT, 1 - 2 * QT)
                    v_.bn_stats(stats[:, 1], y[:, 1]).then_inc(stats_done, 1)
                    v_.bn_aggr(meanvar[:, 0], stats[:, 0]).then_inc(var_done, 1)
                    S.wait(dve, var_done, QT, 1 - 2 * QT)
                    S.wait(dve, stats_done, QT, -QT)
                    link(v_.tensor_scalar(rs_v[:, 0:1], meanvar[:, 0, 1:2], LN_EPS, None, ALU.add), needed=False)
                    v_.bn_aggr(meanvar[:, 1], stats[:, 1]).then_inc(var_done, 1)
                    S.wait(dve, var_done, QT, -QT)
                    link(v_.tensor_scalar(rs_v[:, 1:2], meanvar[:, 1, 1:2], LN_EPS, None, ALU.add))
                    link(v_.tensor_scalar(rs_t[:].bitcast(I32), rs_v[:].bitcast(I32), 1, None, ALU.logical_shift_right))
                    link(v_.tensor_scalar(rs_y[:].bitcast(I32), rs_t[:].bitcast(I32), -1.0, float(0x5F3759DF), ALU.mult, ALU.add))
                    for _ in range(NEWTON):
                        link(v_.scalar_tensor_tensor(rs_t[:], rs_y[:], -0.5, rs_y[:], ALU.mult, ALU.mult))
                        link(v_.tensor_tensor(rs_t[:], rs_t[:], rs_v[:], ALU.mult))
                        link(v_.scalar_tensor_tensor(rs_y[:], rs_t[:], 1.5, rs_y[:], ALU.add, ALU.mult))
                    o = (s - 2) % 2
                    S.wait(dve, st_out[o], 8, -16 - 8 * o)
                    for t in range(QT):
                        v_.tensor_scalar(result[:, o, t], y[:, t], meanvar[:, t, 0:1], rs_y[:, t:t + 1],
                                         ALU.subtract, ALU.mult).then_inc(centred, 1)

                def add_residual():
                    S.wait(dve, pe_o, 1, 0)
                    S.wait(dve, x_biased, 1, 0)
                    S.wait(dve, centred, QT, -QT)
                    v_.tensor_tensor(y[:].rearrange("p t d -> p (t d)"), ps_x[1][:],
                                     x_rows[:, (s - 1) % 2].rearrange("p t d -> p (t d)"), ALU.add).then_inc(y_done, 1)

                def maxima_of(tasks):
                    if S.maxima:
                        for j in tasks:
                            max_of(j)

                maxima_of((0, 1, 2))
                if S.project_q:
                    S.wait(dve, q_hi, 1, 3)
                    query_lo(0, (s // 2 + 1) % 2)
                maxima_of((3, 4, 5))
                if S.project_q:
                    S.wait(dve, q_hi, 1, 4)
                    query_lo(1, (s // 2 + 1) % 2)
                if S.output:
                    normalize()
                maxima_of((6, 7))
                if S.output:
                    S.wait(dve, ctx_hi, 1, 0)
                    S.wait(dve, pe_o, 1, -1)
                    lo(ctx_l[:], ps_x[0][:].rearrange("p (f q) -> p f q", f=HALVES), ctx_h[:]).then_inc(ctx_lo, 1)
                if S.norm:
                    layer_norm()
                if S.output:
                    add_residual()

            all_steps(dve, step)

        @block.gpsimd
        def _(pool):
            g_ = nc.gpsimd
            g_.memset(kblk[:].bitcast(F32), 0.0).then_inc(cleared_k, 1)
            g_.memset(vparts[:, :, :, 0, DK:VW], 1.0).then_inc(cleared_parts, 1)
            g_.memset(vparts[:, :, :, 1:VP, DK:VW], 0.0).then_inc(cleared_parts, 1)
            words = vblk_all[:].bitcast(U32)
            staged = (B - 2) * v_batch // 2
            g_.memset(words[:, 0:staged], 0).then_inc(cleared_v, 1)
            pool.wait_ge(minus_set, 2)
            g_.memset(words[:, staged:], 0).then_inc(cleared_v, 1)

            def step(S):
                s = S.first
                for u in range(UNITS):
                    if S.scores:
                        n = UNITS * s + u
                        S.wait(pool, exp32, UNITS, u + 1)
                        S.wait(pool, exp16, UNITS, u + 1)
                        S.wait(pool, pe_e, UNITS, u + 1 - PSLOTS)
                        g_.tensor_tensor(p_l[:, n % PSLOTS], p32[:, n % P32SLOTS], p_h[:, n % PSLOTS],
                                         ALU.subtract).then_inc(rest16, 1)
                    if u == 0 and S.store:
                        r = result[:, (s - 3) % 2]
                        S.wait(pool, centred, QT, -2 * QT)
                        g_.tensor_tensor(r, r, gamma_sb[:].unsqueeze(1).broadcast_to([P, QT, D]), ALU.mult).then_inc(scaled, 1)
                        S.wait(pool, scaled, 1, -2)
                        g_.tensor_tensor(r, r, beta_sb[:].unsqueeze(1).broadcast_to([P, QT, D]), ALU.add).then_inc(result_done, 1)
                    if u == 2 and S.scores:
                        xr = x_rows[:, s % 2]
                        S.wait(pool, ld_x[s % 2], 8, 16 - 8 * (s % 2))
                        if s == 0:
                            pool.wait_ge(bo_done, 1)
                        g_.tensor_tensor(xr, xr, bo_sb[:].unsqueeze(1).broadcast_to([P, QT, D]), ALU.add).then_inc(x_biased, 1)
                if S.split_x:
                    S.wait(pool, x_hi, 1, 5, by=2)
                    S.wait(pool, pe_q, 1, 3)
                    g_.tensor_tensor(xT_l[:], xT_raw[:], xT_h[:].bitcast(F32), ALU.subtract).then_inc(x_lo, 1)

            all_steps(pool, step)


def kernel(x, ctx_1024, L0_xattn_W_qkv, L0_xattn_b_qkv, L0_xattn_W_o, L0_xattn_b_o, L0_xattn_ln_gamma,
           L0_xattn_ln_beta):
    import numpy as np
    import concourse.bacc as bacc
    from concourse.bass_utils import run_bass_kernel_spmd

    c = np.ascontiguousarray
    w, b = np.asarray(L0_xattn_W_qkv), np.asarray(L0_xattn_b_qkv)
    xr = np.asarray(x).reshape(B * SQ, D)
    minus = np.zeros((MROWS, HALVES, PACKED), np.float32)
    for f in range(HALVES):
        for h in range(HH):
            minus[f * HH + h, f, h * SKV:(h + 1) * SKV] = -1.0
    cut = LOW_TILES * P
    arrays = {
        "xT": c(xr.T), "x": c(xr), "cT": c(np.asarray(ctx_1024).reshape(B * SKV, D).T),
        "wqT": c(w[:D].T), "wkT": c(w[D:2 * D].T), "wvT": c(w[2 * D:].T), "woT": c(np.asarray(L0_xattn_W_o).T),
        "bq": c(b[:D].reshape(HALVES, P).T), "bk": c(b[D:2 * D].reshape(HALVES, P).T),
        "bv": c(b[2 * D:].reshape(KC, P).T), "bo": c(L0_xattn_b_o), "gamma": c(L0_xattn_ln_gamma),
        "beta": c(L0_xattn_ln_beta), "ident": np.eye(P, dtype=np.float32),
        "minus_low": c(minus[:, :, :cut]), "minus_high": c(minus[:, :, cut:]),
    }
    nc = bacc.Bacc("TRN2", target_bir_lowering=False, num_devices=1)
    ins = [nc.dram_tensor(f"in_{k}", list(a.shape), F32, kind="ExternalInput").ap() for k, a in arrays.items()]
    out = nc.dram_tensor("out_dram", [B * SQ, D], F32, kind="ExternalOutput").ap()
    cross_attention_kernel(nc, *ins, out)
    r = run_bass_kernel_spmd(nc, [{f"in_{k}": a for k, a in arrays.items()}], core_ids=[0])
    return r.results[0]["out_dram"].reshape(B, SQ, D)
```

```python
import math
from contextlib import ExitStack

import concourse.bass as bass
from concourse import mybir

F32 = mybir.dt.float32
F32R = mybir.dt.float32r
BF16 = mybir.dt.bfloat16
FP16 = mybir.dt.float16
I32 = mybir.dt.int32
U32 = mybir.dt.uint32
ALU = mybir.AluOpType
ACT = mybir.ActivationFunctionType
AX = mybir.AxisListType

B, SQ, D, SKV, H = 16, 256, 256, 77, 16
DK = D // H
P = 128
HALVES = 2
HH = H // HALVES
KC = D // P
QT = SQ // P
PAIR = 2 * SQ
PACKED = HH * SKV
TILES = -(-PACKED // P)
WIDE = TILES * P
UNITS = HALVES * TILES // 2
DMAX_HEADS = HH // 2
DMAX = QT * HALVES * 2
VW = DK + 1
VP = 3
GROUP = 4
GROUPS = B // GROUP
GK = GROUP * SKV
KSLOTS = 4
PSLOTS = 4
P32SLOTS = 2
MROWS = 32
LOW_TILES = 3
LN_EPS = 1e-5
SCALE = 1.0 / math.sqrt(DK)
EXP_SHIFT = 10 * math.log(2.0)
NEWTON = 3
LOOP_STEPS = 4
LOOPS = 2
LOOP_FIRST = 4
LAST_STEP = B + 2
CHAIN = 3 + 3 * NEWTON


def segments():
    out = []
    for t in range(TILES):
        for h in range(HH):
            a, b = max(P * t, SKV * h), min(P * (t + 1), SKV * (h + 1))
            if a < b:
                out.append((t, h, a - P * t, a - SKV * h, b - a, len(out)))
    return out


SEGMENTS = segments()
NSEG = len(SEGMENTS)


class Step:

    def __init__(self, first, i=None):
        self.first, self.i = first, i
        s = first
        self.scores = 0 <= s < B
        self.maxima = -1 <= s < B - 1
        self.output = 0 <= s - 1 < B
        self.norm = 0 <= s - 2 < B
        self.store = 0 <= s - 3 < B
        self.project_q = s % 2 == 0 and 0 <= s <= B - 4
        self.split_x = s % 2 == 0 and 0 <= s <= B - 6
        self.load_k = s % 2 == 0 and 2 <= s <= B - 4

    def lin(self, a, c, by=1):
        v = (a * self.first + c) // by
        return v if self.i is None else self.i * (a * LOOP_STEPS // by) + v

    def wait(self, eng, sem, a, c, by=1):
        if (a * self.first + c) // by > (0 if self.i is None else -1):
            eng.wait_ge(sem, self.lin(a, c, by))

    def batch(self, tensor, back, axis):
        if self.i is None:
            return tensor[self.first - back] if axis == 0 else tensor[:, self.first - back]
        at = bass.ds(self.lin(1, -back), 1)
        return (tensor[at].squeeze(0) if axis == 0 else tensor[:, at].squeeze(1))


def all_steps(eng, emit):
    for s in range(LOOP_FIRST):
        emit(Step(s))
    with eng.Fori(0, LOOPS) as i:
        for k in range(LOOP_STEPS):
            emit(Step(LOOP_FIRST + k, i))
    for s in range(LOOP_FIRST + LOOPS * LOOP_STEPS, LAST_STEP + 1):
        emit(Step(s))


def cross_attention_kernel(nc, xT, x, cT, wqT, wkT, wvT, woT, bias_cols, bias_rows, ident,
                           minus_low, minus_high, out):
    ctx = ExitStack()
    with ctx:
        def sb(name, shape, dt, stack=ctx):
            return stack.enter_context(nc.sbuf_tensor(name, shape, dt))

        def sem(name):
            return ctx.enter_context(nc.semaphore(name))

        wq_h, wq_l = sb("wq_h", [P, KC, D], F32R), sb("wq_l", [P, KC, D], F32R)
        wo_h, wo_l = sb("wo_h", [P, KC, D], F32R), sb("wo_l", [P, KC, D], F32R)
        kT = sb("kT", [P, B, HALVES, 2, SKV], F32R)
        kblk = sb("kblk", [P, KSLOTS, HALVES, 2, WIDE], F32R)
        vparts = sb("vparts", [SKV, B, H, VP, VW], BF16)
        vblk_all = sb("vblk", [P, B * HALVES * NSEG * VP * VW], BF16)
        vblk = vblk_all[:].rearrange("p (b f n v w) -> p b f n v w", f=HALVES, n=NSEG, v=VP, w=VW)
        xT_raw = sb("xT_raw", [P, KC, PAIR], F32)
        xT_h, xT_l = sb("xT_h", [P, KC, PAIR], F32R), sb("xT_l", [P, KC, PAIR], F32R)
        q_low = [sb(f"q_low{n}", [P, HALVES, PAIR], F32R) for n in range(2)]
        q_high = [sb(f"q_high{n}", [P, HALVES, PAIR], F32R) for n in range(2)]
        q_lo = [sb(f"q_lo{n}", [P, HALVES, PAIR], F32R) for n in range(2)]
        ident_sb = sb("ident_sb", [P, P], F32)
        cols_sb = sb("cols_sb", [P, 3 * HALVES], F32)
        bq_sb, bk_sb, bv_sb = (cols_sb[:, HALVES * n:HALVES * (n + 1)] for n in range(3))
        rows_sb = sb("rows_sb", [P, 3 * D], F32)
        bo_sb, gamma_sb, beta_sb = (rows_sb[:, D * n:D * (n + 1)] for n in range(3))
        maxima = sb("maxima", [P, QT, MROWS], F32)
        shift, warm = sb("shift", [P, 1], F32), sb("warm", [P, 1], F32)
        recip = sb("recip", [P, HALVES, QT, HH], F32)
        stats = sb("stats", [P, QT, 6], F32)
        meanvar = sb("meanvar", [P, QT, 2], F32)
        rs_v, rs_y, rs_t = sb("rs_v", [P, QT], F32), sb("rs_y", [P, 2, QT], F32), sb("rs_t", [P, QT], F32)

        early = ExitStack()
        w_raw = sb("w_raw", [P, 4, KC, D], F32, early)
        wk_h, wk_l = sb("wk_h", [P, KC, D], F32R, early), sb("wk_l", [P, KC, D], F32R, early)
        wv_h, wv_l = sb("wv_h", [P, KC, D], F32R, early), sb("wv_l", [P, KC, D], F32R, early)
        c_raw = sb("c_raw", [P, 2, KC, GK], F32, early)
        c_h, c_l = sb("c_h", [P, 2, KC, GK], F32R, early), sb("c_l", [P, 2, KC, GK], F32R, early)
        vrest = sb("vrest", [SKV, 2, 2, D], F32, early)
        early.close()
        p32 = sb("p32", [P, P32SLOTS, 2, SQ], F32)
        p_h, p_l = sb("p_h", [P, PSLOTS, 2, SQ], FP16), sb("p_l", [P, PSLOTS, 2, SQ], FP16)
        ctx_n = sb("ctx_n", [P, QT, D], F32)
        ctx_h, ctx_l = sb("ctx_h", [P, HALVES, SQ], F32R), sb("ctx_l", [P, HALVES, SQ], F32R)
        y = sb("y", [P, QT, D], F32)
        x_rows = sb("x_rows", [P, 2, QT, D], F32)
        result = sb("result", [P, 2, QT, D], F32)

        def bank(name, shape):
            return ctx.enter_context(nc.psum_tensor(name, shape, F32))

        ps_s = [bank(f"ps_s{n}", [P, 2, SQ]) for n in range(2)]
        ps_acc = [bank(f"ps_acc{n}", [P, 512]) for n in range(2)]
        ps_d = [bank(f"ps_d{n}", [P, 512]) for n in range(2)]
        ps_x = [bank(f"ps_x{n}", [P, 512]) for n in range(2)]

        ld_w = [sem(f"ld_w{n}") for n in range(4)]
        ld_c = [sem(f"ld_c{n}") for n in range(2)]
        ld_cols, ld_rows, ld_ident, ld_minus = sem("ld_cols"), sem("ld_rows"), sem("ld_ident"), sem("ld_minus")
        ld_xT = sem("ld_xT")
        ld_k = [sem(f"ld_k{n}") for n in range(2)]
        ld_v = [sem(f"ld_v{n}") for n in range(2)]
        ld_x = [sem(f"ld_x{n}") for n in range(2)]
        st_out = [sem(f"st_out{n}") for n in range(2)]
        cleared_k, cleared_v, cleared_parts, cleared_m = [sem(f"cleared_k{n}") for n in range(2)], sem("cleared_v"), sem("cleared_parts"), sem("cleared_m")
        minus_set, shift_set = sem("minus_set"), sem("shift_set")
        w_hi, w_lo = sem("w_hi"), sem("w_lo")
        c_hi, c_lo = sem("c_hi"), sem("c_lo")
        bo_done = sem("bo_done")
        pe_bo, pe_k, pe_v = sem("pe_bo"), sem("pe_k"), sem("pe_v")
        k_hi, k_lo = sem("k_hi"), sem("k_lo")
        v_hi, v_rest1, v_mid, v_low = sem("v_hi"), sem("v_rest1"), sem("v_mid"), sem("v_low")
        x_hi, x_lo = sem("x_hi"), sem("x_lo")
        pe_q, q_hi, q_lo_done = sem("pe_q"), sem("q_hi"), sem("q_lo_done")
        pe_d, max_done, pe_m, m_done = sem("pe_d"), sem("max_done"), sem("pe_m"), sem("m_done")
        pe_s, exp16, rest16 = sem("pe_s"), sem("exp16"), sem("rest16")
        pe_e, rec_done, norm_done = sem("pe_e"), sem("rec_done"), sem("norm_done")
        pe_t, ctx_hi, ctx_lo = sem("pe_t"), sem("ctx_hi"), sem("ctx_lo")
        pe_o, x_biased, y_done = sem("pe_o"), sem("x_biased"), sem("y_done")
        stats_done, var_done, newton = sem("stats_done"), sem("var_done"), sem("newton")
        centred, scaled, result_done, finished = sem("centred"), sem("scaled"), sem("result_done"), sem("finished")

        block = ctx.enter_context(nc.Block())

        xT_v = xT.rearrange("(k p) q -> p k q", p=P)
        cT_v = cT.rearrange("(k p) q -> p k q", p=P)
        x_v = x.rearrange("(b t p) d -> b p t d", p=P, t=QT)
        out_v = out.rearrange("(b t p) d -> b p t d", p=P, t=QT)
        WK, WV, WQ, WO = range(4)
        split_w = {WK: (wk_h, wk_l), WQ: (wq_h, wq_l), WV: (wv_h, wv_l), WO: (wo_h, wo_l)}
        V_TASKS = B // 2
        low_rows, high_rows = slice(P - MROWS, P), slice(0, MROWS)
        low_cols, high_cols = LOW_TILES * P, PACKED - LOW_TILES * P
        v_batch = HALVES * NSEG * VP * VW
        stage = vblk_all[:, (B - 2) * v_batch:].bitcast(F32)
        stage_low = stage[low_rows, 0:HALVES * low_cols].rearrange("p (f c) -> p f c", f=HALVES)
        stage_high = stage[high_rows, 0:HALVES * high_cols].rearrange("p (f c) -> p f c", f=HALVES)

        @block.sync
        def _(sp):
            def load_weight(n, w):
                sp.dma_start(w_raw[:, n], w.rearrange("(k p) n -> p k n", p=P)).then_inc(ld_w[n], 16)

            def load_k(batch, slot):
                for h in range(HH):
                    rows = slice(DK * h, DK * (h + 1))
                    sp.dma_start(
                        kblk[rows, 2 * slot:2 * slot + 2, :, :, SKV * h:SKV * (h + 1)].rearrange("p b f l k -> p (b f l) k").bitcast(F32),
                        kT[rows, bass.ds(batch, 2)].rearrange("p b f l k -> p (b f l) k").bitcast(F32)).then_inc(ld_k[slot], 16)

            def load_v(part):
                sp.wait_ge(cleared_v, part + 1)
                for done in (v_hi, v_mid, v_low):
                    sp.wait_ge(done, V_TASKS // 2 * (part + 1))
                b0, b1 = HALVES * B // 2 * part, HALVES * B // 2 * (part + 1)
                src = vparts[:].rearrange("p b (f h) v w -> p (b f) h (v w)", h=HH)
                dst = vblk.rearrange("p b f n v w -> p (b f) n (v w)")
                for t, h, row, key, n, seg in SEGMENTS:
                    sp.dma_start(dst[row:row + n, b0:b1, seg], src[key:key + n, b0:b1, h]).then_inc(ld_v[part], 16)

            load_weight(WK, wkT)
            sp.dma_start(c_raw[:, 0], cT_v[:, :, 0:GK]).then_inc(ld_c[0], 16)
            sp.dma_start(xT_raw[:], xT_v[:, :, 0:PAIR]).then_inc(ld_xT, 16)
            load_weight(WQ, wqT)
            load_weight(WV, wvT)
            sp.dma_start(stage_low, minus_low).then_inc(ld_minus, 16)
            sp.dma_start(stage_high, minus_high).then_inc(ld_minus, 16)
            sp.dma_start(ident_sb[:], ident).then_inc(ld_ident, 16)
            load_weight(WO, woT)
            sp.dma_start(rows_sb[:], bias_rows.partition_broadcast(P)).then_inc(ld_rows, 16)
            sp.wait_ge(x_lo, 1)
            sp.dma_start(xT_raw[:], xT_v[:, :, PAIR:2 * PAIR]).then_inc(ld_xT, 16)
            sp.wait_ge(cleared_k[0], 1)
            sp.wait_ge(cleared_k[1], 1)
            sp.wait_ge(k_lo, HALVES)
            load_k(0, 0)
            load_v(0)
            sp.wait_ge(cleared_k[1], 2)
            load_k(2, 1)

            def step(S):
                s = S.first
                if s == 1:
                    load_v(1)
                if S.split_x:
                    S.wait(sp, x_lo, 1, 4, by=2)
                    sp.dma_start(xT_raw[:], xT_v[:, :, bass.ds(S.lin(SQ, 4 * SQ), PAIR)]).then_inc(ld_xT, 16)
                if S.load_k:
                    if s == 2:
                        sp.wait_ge(k_lo, HALVES * GROUPS)
                    S.wait(sp, pe_s, UNITS, 0)
                    load_k(S.lin(1, 2), (s // 2 + 1) % 2)
                if S.scores:
                    if s == 0:
                        sp.wait_ge(pe_v, V_TASKS)
                        sp.wait_ge(pe_bo, 1)
                    S.wait(sp, y_done, 1, -1)
                    sp.dma_start(x_rows[:, s % 2], S.batch(x_v, 0, 0)).then_inc(ld_x[s % 2], 16)
                if S.store:
                    if s < LAST_STEP:
                        S.wait(sp, result_done, 1, -2)
                    else:
                        sp.wait_ge(finished, QT)
                    sp.dma_start(S.batch(out_v, 3, 0), result[:, (s - 3) % 2]).then_inc(st_out[(s - 3) % 2], 16)

            all_steps(sp, step)
            for n in range(2):
                sp.wait_ge(st_out[n], 16 * B // 2)

        @block.tensor
        def _(pe):
            def mm(o, w, m, start, stop):
                return nc.tensor.matmul(o, w, m, start=start, stop=stop, skip_group_check=True)

            def three(o, w, m):
                terms = [(a, b, k) for k in range(KC) for a, b in ((0, 0), (0, 1), (1, 0))]
                for n, (a, b, k) in enumerate(terms):
                    ins = mm(o, w(a, k), m(b, k), n == 0, n == len(terms) - 1)
                return ins

            def project_k(g):
                pe.wait_ge(c_lo, g + 1)
                for f in range(HALVES):
                    if g:
                        pe.wait_ge(k_lo, HALVES * (g - 1) + f + 1)
                    three(ps_x[f][:, 0:GK], lambda a, k: (wk_h, wk_l)[a][:, k, f * P:(f + 1) * P],
                          lambda b, k: (c_h, c_l)[b][:, g % 2, k, :]).then_inc(pe_k, 1)

            def project_v(g, n):
                if g:
                    pe.wait_ge(v_rest1, 2 * g + n - 1)
                for j in range(2):
                    at = (2 * n + j) * SKV
                    ins = three(ps_acc[n][0:SKV, j * D:(j + 1) * D],
                                lambda a, k: (c_h, c_l)[a][:, g % 2, k, at:at + SKV],
                                lambda b, k: (wv_h, wv_l)[b][:, k, :])
                ins.then_inc(pe_v, 1)

            def project_q(f):
                three(ps_x[f][:], lambda a, k: (wq_h, wq_l)[a][:, k, f * P:(f + 1) * P],
                      lambda b, k: (xT_h, xT_l)[b][:, k, :]).then_inc(pe_q, 1)

            pe.wait_ge(w_lo, 1)
            project_k(0)
            pe.wait_ge(w_lo, 2)
            pe.wait_ge(x_lo, 1)
            for f in range(HALVES):
                pe.wait_ge(k_lo, f + 1)
                project_q(f)
            pe.wait_ge(w_lo, 3)
            project_v(0, 0)
            project_v(0, 1)

            def step(S, between={}):
                s = S.first
                nb = s + 1

                def max_bank(j):
                    return ps_d[((DMAX + 1) * nb + j) % 2]

                def max_scores(j):
                    t, f, n = j // 4, j // 2 % 2, j % 2
                    if j == 0:
                        if nb % 2 == 0:
                            S.wait(pe, ld_k[nb // 2 % 2], 16 * HH, 16 * HH * (5 - nb % 4), by=4)
                            S.wait(pe, q_hi, 1, 3)
                        S.wait(pe, max_done, DMAX, DMAX)
                    elif j == 1:
                        S.wait(pe, m_done, 1, 1)
                    else:
                        S.wait(pe, max_done, DMAX, DMAX + j - 1)
                    q0 = nb % 2 * SQ + t * P
                    mm(max_bank(j)[:, 0:DMAX_HEADS * SKV], q_low[nb // 2 % 2][:, f, q0:q0 + P],
                       kblk[:, nb % KSLOTS, f, 0, n * DMAX_HEADS * SKV:(n + 1) * DMAX_HEADS * SKV],
                       True, True).then_inc(pe_d, 1)

                def turn_maxima():
                    S.wait(pe, max_done, DMAX, 2 * DMAX)
                    for t in range(QT):
                        ins = nc.tensor.transpose(max_bank(DMAX)[0:MROWS, t * P:(t + 1) * P], maxima[:, t, :], ident_sb[:])
                    ins.then_inc(pe_m, 1)

                def score_tile(u, n):
                    f, t = divmod(2 * u + n, TILES)
                    if n == 0:
                        S.wait(pe, exp16, UNITS, u - 1)
                        if s == 0 and u == 1:
                            pe.wait_ge(bo_done, 1)
                    if u == 0 and n == 0:
                        S.wait(pe, m_done, 1, 1)
                        S.wait(pe, q_lo_done, 1, 2 - s % 2)
                        if s == 0:
                            pe.wait_ge(minus_set, 2)
                    tile = slice(t * P, (t + 1) * P)
                    cols = slice(s % 2 * SQ, (s % 2 + 1) * SQ)
                    q = (q_low if t < LOW_TILES else q_high)[s // 2 % 2][:, f, cols]
                    o = ps_s[(UNITS * s + u) % 2][:, n, :]
                    mm(o, kblk[:, s % KSLOTS, f, 0, tile], q, True, False)
                    mm(o, kblk[:, s % KSLOTS, f, 0, tile], q_lo[s // 2 % 2][:, f, cols], False, False)
                    ins = mm(o, kblk[:, s % KSLOTS, f, 1, tile], q, False, True)
                    if n == 1:
                        ins.then_inc(pe_s, 1)

                def weigh(u, n, back):
                    g = 2 * u + n
                    f, t = divmod(g, TILES)
                    slot = (UNITS * (s - back) + u) % PSLOTS
                    heads = [x[1] for x in SEGMENTS if x[0] == t]
                    s0 = [x[5] for x in SEGMENTS if x[0] == t][0]
                    if n == 0:
                        S.wait(pe, rest16, UNITS, u + 1 - UNITS * back)
                    if t == 0:
                        S.wait(pe, norm_done, HALVES, f + 1 - HALVES * (back + 1))
                    if g == 0:
                        if s == LOOP_FIRST - 1:
                            pe.wait_ge(ld_v[1], 16 * NSEG)
                        if s == 0:
                            pe.wait_ge(ld_v[0], 16 * NSEG)
                            pe.wait_ge(v_rest1, V_TASKS)
                    for qt in range(QT):
                        at = (qt * HH + heads[0]) * VW
                        o = ps_acc[f][:, at:at + len(heads) * VW].rearrange("p (n w) -> p n w", w=VW)
                        for j, (p, v) in enumerate(((p_h, 0), (p_h, 1), (p_h, 2), (p_l, 0), (p_l, 1))):
                            ins = mm(o, p[:, slot, n, qt * P:(qt + 1) * P],
                                     S.batch(vblk, back, 1)[:, f, s0:s0 + len(heads), v, :],
                                     t == 0 and qt == 0 and j == 0, t == TILES - 1 and qt == QT - 1 and j == 4)
                    if n == 1:
                        ins.then_inc(pe_e, 1)

                def turn_context():
                    S.wait(pe, norm_done, HALVES, 0)
                    if S.project_q:
                        S.wait(pe, q_lo_done, 1, 3)
                    else:
                        S.wait(pe, ctx_lo, 1, -1)
                    for f in range(HALVES):
                        for qt in range(QT):
                            ins = nc.tensor.transpose(ps_x[0][:, f * SQ + qt * P:f * SQ + (qt + 1) * P],
                                                      ctx_n[:, qt, f * P:(f + 1) * P], ident_sb[:])
                    ins.then_inc(pe_t, 1)

                def project_out():
                    S.wait(pe, ctx_lo, 1, 0)
                    if S.project_q:
                        S.wait(pe, q_lo_done, 1, 4)
                    else:
                        S.wait(pe, y_done, 1, -1)
                    if s == 1:
                        pe.wait_ge(w_lo, 4)
                    for qt in range(QT):
                        ins = three(ps_x[1][:, qt * D:(qt + 1) * D],
                                    lambda a, k: (ctx_h, ctx_l)[a][:, k, qt * P:(qt + 1) * P],
                                    lambda b, k: (wo_h, wo_l)[b][:, k, :])
                    ins.then_inc(pe_o, 1)

                def next_q(f):
                    if s == 0:
                        pe.wait_ge(k_lo, HALVES * (GROUPS - 1) + f + 1)
                    if f == 0:
                        S.wait(pe, x_lo, 1, 4, by=2)
                        S.wait(pe, ctx_lo, 1, -1)
                    else:
                        S.wait(pe, y_done, 1, -1)
                    project_q(f)

                tasks = {(0, 0): 0, (0, 1): 1, (1, 0): 2, (1, 1): 3, (2, 0): 4, (2, 1): 5, (3, 0): 6, (3, 1): 7,
                         (4, 1): DMAX}
                for u in range(UNITS):
                    for part in range(4):
                        if part < 2 and S.scores:
                            score_tile(u, part)
                        if part >= 2 and u < 2 and S.output:
                            weigh(u + 3, part - 2, 1)
                        if part >= 2 and u >= 2 and S.scores:
                            weigh(u - 2, part - 2, 0)
                        if (u, part) == (3, 1) and S.output:
                            turn_context()
                        if (u, part) in tasks and S.maxima:
                            j = tasks[u, part]
                            max_scores(j) if j < DMAX else turn_maxima()
                    if u < 2 and S.project_q:
                        next_q(u)
                    if u == 4 and S.output:
                        project_out()
                    if u in between:
                        between[u]()

            def project_bias():
                for k in range(KC):
                    ins = mm(ps_s[1][:, 0, :], bv_sb[:, k:k + 1].to_broadcast([P, P]), w_raw[:, WO, k, :], k == 0, k == KC - 1)
                ins.then_inc(pe_bo, 1)

            pe.wait_ge(q_lo_done, HALVES)
            project_k(1)
            project_v(1, 0)
            pe.wait_ge(cleared_m, 1)
            pe.wait_ge(ld_ident, 16)
            pe.wait_ge(ld_cols, 16)
            pe.wait_ge(ld_w[WO], 16)
            step(Step(-1), {0: lambda: project_v(1, 1), 1: project_bias, 2: lambda: project_k(2),
                            3: lambda: project_v(2, 0)})
            project_v(2, 1)
            project_k(3)
            project_v(3, 0)
            project_v(3, 1)
            all_steps(pe, step)

        @block.scalar
        def _(act):
            copy, add = ACT.Copy, ACT.Identity
            weights = list(split_w.items())

            def load_context(g):
                act.dma_start(c_raw[:, g % 2], cT_v[:, :, g * GK:(g + 1) * GK]).then_inc(ld_c[g % 2], 16)

            act.wait_ge(shift_set, 1)
            nc.scalar.activation(warm[:], shift[:], ACT.Exp)
            act.dma_start(cols_sb[:], bias_cols).then_inc(ld_cols, 16)
            load_context(1)

            def weight_hi(n):
                w, (hi, _) = weights[n]
                act.wait_ge(ld_w[w], 16)
                nc.scalar.activation(hi[:], w_raw[:, w], copy).then_inc(w_hi, 1)

            def context_hi(g):
                act.wait_ge(ld_c[g % 2], 16 * (g // 2 + 1))
                if g >= 2:
                    act.wait_ge(pe_v, 2 * (g - 1))
                nc.scalar.activation(c_h[:, g % 2], c_raw[:, g % 2], copy).then_inc(c_hi, 1)

            def key_hi(g):
                for f in range(HALVES):
                    act.wait_ge(pe_k, HALVES * g + f + 1)
                    nc.scalar.activation(kT[:, GROUP * g:GROUP * (g + 1), f, 0, :],
                                         ps_x[f][:, 0:GK].rearrange("p (b k) -> p b k", k=SKV), add,
                                         bias=bk_sb[:, f:f + 1]).then_inc(k_hi, 1)

            def value_part(v, part):
                return vparts[:, 2 * v:2 * v + 2, :, part, 0:DK].rearrange("p b h w -> p (b h) w")

            def value_hi(v):
                act.wait_ge(pe_v, v + 1)
                nc.scalar.activation(value_part(v, 0), ps_acc[v % 2][0:SKV, :].rearrange("p (n w) -> p n w", w=DK),
                                     copy).then_inc(v_hi, 1)

            def value_mid(v):
                act.wait_ge(v_rest1, v + 1)
                nc.scalar.activation(value_part(v, 1), vrest[:, v % 2].rearrange("p b (h w) -> p (b h) w", w=DK),
                                     copy).then_inc(v_mid, 1)

            def query_hi(f, slot):
                nc.scalar.activation(q_low[slot][:, f], ps_x[f][:], add, bias=bq_sb[:, f:f + 1])
                nc.scalar.activation(q_high[slot][:, f], ps_x[f][:], add, bias=bq_sb[:, f:f + 1]).then_inc(q_hi, 1)

            def split_x():
                nc.scalar.activation(xT_h[:], xT_raw[:], copy).then_inc(x_hi, 1)

            weight_hi(0)
            context_hi(0)
            weight_hi(1)
            act.wait_ge(ld_xT, 16)
            split_x()
            weight_hi(2)
            act.wait_ge(ld_cols, 16)
            key_hi(0)
            context_hi(1)
            for f in range(HALVES):
                act.wait_ge(pe_q, f + 1)
                query_hi(f, 0)
            act.wait_ge(c_lo, 1)
            load_context(2)

            def step(S):
                s = S.first

                def exponentials(u):
                    S.wait(act, pe_s, UNITS, u + 1)
                    S.wait(act, rest16, UNITS, u + 1 - P32SLOTS)
                    S.wait(act, pe_e, UNITS, u + 1 - PSLOTS)
                    if s == 0 and u == 0:
                        act.wait_ge(pe_bo, 1)
                        act.wait_ge(w_lo, 4)
                    n = UNITS * s + u
                    nc.scalar.activation(p32[:, n % P32SLOTS], ps_s[n % 2][:], ACT.Exp, scale=SCALE)
                    nc.scalar.activation(p_h[:, n % PSLOTS], ps_s[n % 2][:], ACT.Exp, scale=SCALE).then_inc(exp16, 1)

                def write_maxima():
                    S.wait(act, pe_m, 1, 2)
                    if s == -1:
                        act.wait_ge(shift_set, 1)
                    nb = s + 1
                    cols = slice(nb % 2 * SQ, (nb % 2 + 1) * SQ)
                    m = ps_d[((DMAX + 1) * nb + DMAX) % 2][0:MROWS, 0:SQ].unsqueeze(1).broadcast_to([MROWS, HALVES, SQ])
                    nc.scalar.activation(q_low[nb // 2 % 2][low_rows, :, cols], m, add, bias=shift[low_rows, 0:1])
                    nc.scalar.activation(q_high[nb // 2 % 2][high_rows, :, cols], m, add,
                                         bias=shift[high_rows, 0:1]).then_inc(m_done, 1)

                for u in range(UNITS):
                    if u == 4 and S.maxima:
                        write_maxima()
                    if S.scores:
                        exponentials(u)
                    if u < HALVES and S.project_q:
                        S.wait(act, pe_q, 1, 3 + u)
                        S.wait(act, pe_s, UNITS, 0)
                        query_hi(u, (s // 2 + 1) % 2)
                    if u == 1 and S.store and s < LAST_STEP:
                        S.wait(act, newton, CHAIN, -2 * CHAIN)
                        S.wait(act, centred, QT, -2 * QT)
                        for t in range(QT):
                            r = result[:, (s - 3) % 2, t]
                            nc.scalar.activation(r, r, copy, scale=rs_y[:, (s - 3) % 2, t:t + 1]).then_inc(scaled, 1)
                    if u == 3 and S.output:
                        S.wait(act, pe_t, 1, 0)
                        S.wait(act, pe_o, 1, -1)
                        nc.scalar.activation(ctx_h[:], ps_x[0][:].rearrange("p (f q) -> p f q", f=HALVES),
                                             copy).then_inc(ctx_hi, 1)
                    if u == 3 and S.split_x:
                        S.wait(act, ld_xT, 8, 8 * 6)
                        S.wait(act, pe_q, 1, 4)
                        split_x()

            def values(g):
                value_hi(2 * g)
                value_hi(2 * g + 1)
                value_mid(2 * g)
                value_mid(2 * g + 1)

            values(0)
            key_hi(1)
            context_hi(2)
            act.wait_ge(c_lo, 2)
            load_context(3)
            values(1)
            act.wait_ge(ld_xT, 32)
            act.wait_ge(pe_q, HALVES)
            split_x()
            key_hi(2)
            context_hi(3)
            weight_hi(3)
            value_hi(4)
            value_hi(5)
            value_mid(4)
            value_mid(5)
            step(Step(-1))
            key_hi(3)
            values(3)
            all_steps(act, step)

        @block.vector
        def _(dve):
            weights = list(split_w.items())
            v_ = nc.vector

            def lo(out_, whole, hi):
                return v_.tensor_tensor(out_, whole, hi.bitcast(F32), ALU.subtract)

            def lo_biased(out_, whole, bias, hi):
                return v_.scalar_tensor_tensor(out_, whole, bias, hi.bitcast(F32), ALU.add, ALU.subtract)

            v_.memset(shift[:], -EXP_SHIFT / SCALE).then_inc(shift_set, 1)
            v_.memset(kblk[:, 0].bitcast(F32), 0.0).then_inc(cleared_k[0], 1)
            v_.memset(maxima[:], 0.0).then_inc(cleared_m, 1)

            def weight_lo(n):
                w, (hi, low) = weights[n]
                dve.wait_ge(w_hi, n + 1)
                lo(low[:], w_raw[:, w], hi[:]).then_inc(w_lo, 1)

            def context_lo(g):
                dve.wait_ge(c_hi, g + 1)
                lo(c_l[:, g % 2], c_raw[:, g % 2], c_h[:, g % 2]).then_inc(c_lo, 1)

            def key_lo(g):
                for f in range(HALVES):
                    dve.wait_ge(k_hi, HALVES * g + f + 1)
                    part = kT[:, GROUP * g:GROUP * (g + 1), f]
                    lo_biased(part[:, :, 1, :], ps_x[f][:, 0:GK].rearrange("p (b k) -> p b k", k=SKV),
                              bk_sb[:, f:f + 1], part[:, :, 0, :]).then_inc(k_lo, 1)

            def value_part(v, part):
                return vparts[:, 2 * v:2 * v + 2, :, part, 0:DK].rearrange("p b h w -> p (b h) w")

            def value_rest(v):
                dve.wait_ge(v_hi, v + 1)
                if v >= 2:
                    dve.wait_ge(v_low, v - 1)
                v_.tensor_tensor(vrest[:, v % 2].rearrange("p b (h w) -> p (b h) w", w=DK),
                                 ps_acc[v % 2][0:SKV, :].rearrange("p (n w) -> p n w", w=DK),
                                 value_part(v, 0), ALU.subtract).then_inc(v_rest1, 1)

            def query_lo(f, slot):
                lo_biased(q_lo[slot][:, f], ps_x[f][:], bq_sb[:, f:f + 1], q_high[slot][:, f]).then_inc(q_lo_done, 1)

            def split_x():
                lo(xT_l[:], xT_raw[:], xT_h[:]).then_inc(x_lo, 1)

            weight_lo(0)
            context_lo(0)
            weight_lo(1)
            dve.wait_ge(x_hi, 1)
            split_x()
            dve.wait_ge(ld_cols, 16)
            key_lo(0)
            weight_lo(2)
            context_lo(1)
            for f in range(HALVES):
                dve.wait_ge(q_hi, f + 1)
                query_lo(f, 0)

            def step(S, between={}):
                s = S.first

                def accumulated(f):
                    return ps_acc[f][:, 0:QT * HH * VW].rearrange("p (t h w) -> p t h w", t=QT, w=VW)

                def max_of(j):
                    t, f, n = j // 4, j // 2 % 2, j % 2
                    S.wait(dve, pe_d, DMAX, DMAX + j + 1)
                    if j == 0:
                        S.wait(dve, pe_m, 1, 1)
                    h0 = f * HH + n * DMAX_HEADS
                    v_.tensor_reduce(maxima[:, t, h0:h0 + DMAX_HEADS],
                                     ps_d[((DMAX + 1) * (s + 1) + j) % 2][:, 0:DMAX_HEADS * SKV]
                                     .rearrange("p (h k) -> p h k", k=SKV), AX.X, ALU.max).then_inc(max_done, 1)
                    if j in between:
                        between[j]()

                def denominators(f):
                    S.wait(dve, pe_e, UNITS, 0 if f else UNITS // 2 + 1 - UNITS)
                    v_.reciprocal(recip[:, f], accumulated(f)[:, :, :, DK]).then_inc(rec_done, 1)

                def normalize(f):
                    S.wait(dve, rec_done, HALVES, f + 1 - HALVES)
                    if f == 0:
                        S.wait(dve, pe_t, 1, -1)
                    v_.tensor_tensor(ctx_n[:, :, f * P:(f + 1) * P].rearrange("p t (h w) -> p t h w", w=DK),
                                     accumulated(f)[:, :, :, 0:DK],
                                     recip[:, f].unsqueeze(3).broadcast_to([P, QT, HH, DK]),
                                     ALU.mult).then_inc(norm_done, 1)

                def residual():
                    S.wait(dve, pe_o, 1, -1)
                    S.wait(dve, x_biased, 1, -1)
                    S.wait(dve, centred, QT, -2 * QT)
                    v_.tensor_tensor(y[:].rearrange("p t d -> p (t d)"), ps_x[1][:],
                                     x_rows[:, s % 2].rearrange("p t d -> p (t d)"), ALU.add).then_inc(y_done, 1)
                    S.wait(dve, y_done, 1, -1)

                def statistics(t):
                    v_.bn_stats(stats[:, t], y[:, t]).then_inc(stats_done, 1)

                def aggregate():
                    for t in range(QT):
                        v_.bn_aggr(meanvar[:, t], stats[:, t]).then_inc(var_done, 1)

                root = rs_y[:, s % 2]
                guess = [
                    lambda: v_.tensor_scalar(rs_v[:], meanvar[:, :, 1], LN_EPS, None, ALU.add),
                    lambda: v_.tensor_scalar(rs_t[:].bitcast(I32), rs_v[:].bitcast(I32), 1, None,
                                             ALU.logical_shift_right),
                    lambda: v_.tensor_scalar(root.bitcast(I32), rs_t[:].bitcast(I32), -1.0, float(0x5F3759DF),
                                             ALU.mult, ALU.add)]
                newton_step = [
                    lambda: v_.scalar_tensor_tensor(rs_t[:], root, -0.5, root, ALU.mult, ALU.mult),
                    lambda: v_.tensor_tensor(rs_t[:], rs_t[:], rs_v[:], ALU.mult),
                    lambda: v_.scalar_tensor_tensor(root, rs_t[:], 1.5, root, ALU.add, ALU.mult)]
                chain = guess + NEWTON * newton_step

                def small(n):
                    if n == 0:
                        S.wait(dve, var_done, QT, -QT)
                    else:
                        S.wait(dve, newton, CHAIN, n - 2 * CHAIN)
                    if n == 2:
                        S.wait(dve, scaled, QT, -3 * QT)
                    chain[n]().then_inc(newton, 1)

                def centre(t):
                    o = s % 2
                    if t == 0:
                        S.wait(dve, st_out[o], 8, -16 - 8 * o)
                    v_.scalar_tensor_tensor(result[:, o, t], y[:, t], meanvar[:, t, 0:1], gamma_sb,
                                            ALU.subtract, ALU.mult).then_inc(centred, 1)

                def context_lo_part():
                    S.wait(dve, ctx_hi, 1, 0)
                    S.wait(dve, pe_o, 1, -1)
                    lo(ctx_l[:], ps_x[0][:].rearrange("p (f q) -> p f q", f=HALVES), ctx_h[:]).then_inc(ctx_lo, 1)

                def queries(f):
                    S.wait(dve, q_hi, 1, 3 + f)
                    query_lo(f, (s // 2 + 1) % 2)

                def when(on, *what):
                    if on:
                        for fn, *args in what:
                            fn(*args)

                when(S.output, (denominators, 0))
                when(S.maxima, (max_of, 0))
                when(S.output, (normalize, 0))
                when(S.maxima, (max_of, 1))
                when(S.norm, (residual,))
                when(S.maxima, (max_of, 2))
                when(S.norm, (statistics, 0))
                when(S.project_q, (queries, 0))
                when(S.maxima, (max_of, 3))
                when(S.norm, (statistics, 1))
                when(S.output, (denominators, 1))
                if S.norm:
                    S.wait(dve, stats_done, QT, -QT)
                when(S.maxima, (max_of, 4))
                when(S.norm, (aggregate,))
                when(S.output, (normalize, 1))
                when(S.norm, (small, 0))
                when(S.project_q, (queries, 1))
                when(S.norm, (small, 1))
                when(S.maxima, (max_of, 5))
                when(S.norm, (small, 2))
                when(S.maxima, (max_of, 6))
                when(S.norm, (small, 3))
                when(S.norm, (small, 4))
                when(S.maxima, (max_of, 7))
                when(S.norm, (small, 5))
                if S.split_x:
                    when(S.norm, (centre, 0), (small, 6), (centre, 1))
                    when(S.output, (context_lo_part,))
                    when(S.norm, (small, 7))
                    S.wait(dve, x_hi, 1, 6, by=2)
                    split_x()
                    when(S.norm, *((small, n) for n in range(8, CHAIN)))
                else:
                    when(S.output, (context_lo_part,))
                    when(S.norm, (small, 6), (centre, 0), (small, 7), (centre, 1))
                    when(S.norm, *((small, n) for n in range(8, CHAIN)))
                if s == LAST_STEP - 1:
                    dve.wait_ge(newton, CHAIN * B)
                    for t in range(QT):
                        r = result[:, (B - 1) % 2, t]
                        v_.scalar_tensor_tensor(r, r, root[:, t:t + 1], beta_sb, ALU.mult, ALU.add).then_inc(finished, 1)

            def values(g):
                value_rest(2 * g)
                value_rest(2 * g + 1)

            def set_minus():
                dve.wait_ge(cleared_k[0], 1)
                dve.wait_ge(cleared_k[1], 2)
                dve.wait_ge(ld_minus, 32)
                v_.tensor_copy(kblk[low_rows, :, :, 1, 0:low_cols],
                               stage_low.unsqueeze(1).broadcast_to([MROWS, KSLOTS, HALVES, low_cols])).then_inc(minus_set, 1)
                v_.tensor_copy(kblk[high_rows, :, :, 1, low_cols:PACKED],
                               stage_high.unsqueeze(1).broadcast_to([MROWS, KSLOTS, HALVES, high_cols])).then_inc(minus_set, 1)

            def output_bias():
                dve.wait_ge(ld_rows, 16)
                dve.wait_ge(pe_bo, 1)
                v_.tensor_tensor(bo_sb, ps_s[1][:, 0, :], bo_sb, ALU.add).then_inc(bo_done, 1)

            def split_second_x():
                dve.wait_ge(x_hi, 2)
                split_x()

            values(0)
            key_lo(1)
            step(Step(-1), {1: lambda: values(1), 3: lambda: context_lo(2), 5: split_second_x,
                            7: lambda: (key_lo(2), context_lo(3))})
            values(2)
            set_minus()
            weight_lo(3)
            output_bias()
            key_lo(3)
            values(3)
            all_steps(dve, step)

        @block.gpsimd
        def _(pool):
            g_ = nc.gpsimd
            g_.memset(kblk[:, 1].bitcast(F32), 0.0).then_inc(cleared_k[1], 1)
            g_.memset(kblk[:, 2:KSLOTS].bitcast(F32), 0.0).then_inc(cleared_k[1], 1)
            g_.memset(vparts[:, :, :, 0, DK:VW], 1.0).then_inc(cleared_parts, 1)
            g_.memset(vparts[:, :, :, 1:VP, DK:VW], 0.0).then_inc(cleared_parts, 1)
            words = vblk_all[:].bitcast(U32)
            staged = (B - 2) * v_batch // 2

            def value_low(v):
                pool.wait_ge(v_mid, v + 1)
                g_.tensor_tensor(vparts[:, 2 * v:2 * v + 2, :, 2, 0:DK].rearrange("p b h w -> p (b h) w"),
                                 vrest[:, v % 2].rearrange("p b (h w) -> p (b h) w", w=DK),
                                 vparts[:, 2 * v:2 * v + 2, :, 1, 0:DK].rearrange("p b h w -> p (b h) w"),
                                 ALU.subtract).then_inc(v_low, 1)

            g_.memset(words[:, 0:staged], 0).then_inc(cleared_v, 1)
            for v in range(V_TASKS):
                value_low(v)
                if v == V_TASKS - 3:
                    pool.wait_ge(minus_set, 2)
                    g_.memset(words[:, staged:], 0).then_inc(cleared_v, 1)

            def step(S):
                s = S.first
                for u in range(UNITS):
                    if S.scores:
                        n = UNITS * s + u
                        S.wait(pool, exp16, UNITS, u + 1)
                        if s == 0 and u == 0:
                            pool.wait_ge(pe_k, HALVES * GROUPS)
                        g_.tensor_tensor(p_l[:, n % PSLOTS], p32[:, n % P32SLOTS], p_h[:, n % PSLOTS],
                                         ALU.subtract).then_inc(rest16, 1)
                    if u == 2 and S.store and s < LAST_STEP:
                        r = result[:, (s - 3) % 2]
                        S.wait(pool, scaled, QT, -2 * QT)
                        g_.tensor_tensor(r, r, beta_sb.unsqueeze(1).broadcast_to([P, QT, D]),
                                         ALU.add).then_inc(result_done, 1)
                    if u == 4 and S.scores:
                        xr = x_rows[:, s % 2]
                        S.wait(pool, ld_x[s % 2], 8, 16 - 8 * (s % 2))
                        if s == 0:
                            pool.wait_ge(bo_done, 1)
                        g_.tensor_tensor(xr, xr, bo_sb.unsqueeze(1).broadcast_to([P, QT, D]), ALU.add).then_inc(x_biased, 1)

            all_steps(pool, step)


def kernel(x, ctx_1024, L0_xattn_W_qkv, L0_xattn_b_qkv, L0_xattn_W_o, L0_xattn_b_o, L0_xattn_ln_gamma,
           L0_xattn_ln_beta):
    import numpy as np
    import concourse.bacc as bacc
    from concourse.bass_utils import run_bass_kernel_spmd

    c = np.ascontiguousarray
    w, b = np.asarray(L0_xattn_W_qkv), np.asarray(L0_xattn_b_qkv)
    xr = np.asarray(x).reshape(B * SQ, D)
    minus = np.zeros((MROWS, HALVES, PACKED), np.float32)
    for f in range(HALVES):
        for h in range(HH):
            minus[f * HH + h, f, h * SKV:(h + 1) * SKV] = -1.0
    cut = LOW_TILES * P
    arrays = {
        "xT": c(xr.T), "x": c(xr), "cT": c(np.asarray(ctx_1024).reshape(B * SKV, D).T),
        "wqT": c(w[:D].T), "wkT": c(w[D:2 * D].T), "wvT": c(w[2 * D:].T), "woT": c(np.asarray(L0_xattn_W_o).T),
        "bias_cols": c(b.reshape(3 * HALVES, P).T),
        "bias_rows": c(np.concatenate([np.asarray(L0_xattn_b_o), np.asarray(L0_xattn_ln_gamma),
                                       np.asarray(L0_xattn_ln_beta)])), "ident": np.eye(P, dtype=np.float32),
        "minus_low": c(minus[:, :, :cut]), "minus_high": c(minus[:, :, cut:]),
    }
    nc = bacc.Bacc("TRN2", target_bir_lowering=False, num_devices=1)
    ins = [nc.dram_tensor(f"in_{k}", list(a.shape), F32, kind="ExternalInput").ap() for k, a in arrays.items()]
    out = nc.dram_tensor("out_dram", [B * SQ, D], F32, kind="ExternalOutput").ap()
    cross_attention_kernel(nc, *ins, out)
    r = run_bass_kernel_spmd(nc, [{f"in_{k}": a for k, a in arrays.items()}], core_ids=[0])
    return r.results[0]["out_dram"].reshape(B, SQ, D)
```

```python
import math
from contextlib import ExitStack

import concourse.bass as bass
from concourse import mybir

F32 = mybir.dt.float32
F32R = mybir.dt.float32r
BF16 = mybir.dt.bfloat16
FP16 = mybir.dt.float16
I32 = mybir.dt.int32
U32 = mybir.dt.uint32
ALU = mybir.AluOpType
ACT = mybir.ActivationFunctionType
AX = mybir.AxisListType

B, SQ, D, SKV, H = 16, 256, 256, 77, 16
DK = D // H
P = 128
HALVES = 2
HH = H // HALVES
KC = D // P
QT = SQ // P
PAIR = 2 * SQ
PACKED = HH * SKV
TILES = -(-PACKED // P)
WIDE = TILES * P
UNITS = HALVES * TILES // 2
DMAX_HEADS = HH // 2
DMAX = QT * HALVES * 2
VW = DK + 1
VP = 3
GROUP = 4
GROUPS = B // GROUP
GK = GROUP * SKV
KSLOTS = 4
PSLOTS = 4
P32SLOTS = 2
MROWS = 32
LOW_TILES = 3
MIX_LOW = SKV * HH // 2 // P * P
MIX_HIGH = -(-SKV * HH // 2 // P) * P
LN_EPS = 1e-5
SCALE = 1.0 / math.sqrt(DK)
EXP_SHIFT = 10 * math.log(2.0)
NEWTON = 3
LOOP_STEPS = 4
LOOPS = 2
LOOP_FIRST = 4
LAST_STEP = B + 2
CHAIN = 3 + 3 * NEWTON


def segments():
    out = []
    for t in range(TILES):
        for h in range(HH):
            a, b = max(P * t, SKV * h), min(P * (t + 1), SKV * (h + 1))
            if a < b:
                out.append((t, h, a - P * t, a - SKV * h, b - a, len(out)))
    return out


SEGMENTS = segments()
NSEG = len(SEGMENTS)


class Step:

    def __init__(self, first, i=None):
        self.first, self.i = first, i
        s = first
        self.scores = 0 <= s < B
        self.maxima = -1 <= s < B - 1
        self.output = 0 <= s - 1 < B
        self.norm = 0 <= s - 2 < B
        self.store = 0 <= s - 3 < B
        self.project_q = s % 2 == 0 and 0 <= s <= B - 4
        self.load_x = s % 2 == 0 and 0 <= s <= B - 6
        self.split_x = s % 2 == 1 and 1 <= s <= B - 5
        self.load_k = s % 2 == 0 and 2 <= s <= B - 4

    def lin(self, a, c, by=1):
        v = (a * self.first + c) // by
        return v if self.i is None else self.i * (a * LOOP_STEPS // by) + v

    def wait(self, eng, sem, a, c, by=1):
        if (a * self.first + c) // by > (0 if self.i is None else -1):
            eng.wait_ge(sem, self.lin(a, c, by))

    def batch(self, tensor, back, axis):
        if self.i is None:
            return tensor[self.first - back] if axis == 0 else tensor[:, self.first - back]
        at = bass.ds(self.lin(1, -back), 1)
        return (tensor[at].squeeze(0) if axis == 0 else tensor[:, at].squeeze(1))


def all_steps(eng, emit):
    for s in range(LOOP_FIRST):
        emit(Step(s))
    with eng.Fori(0, LOOPS) as i:
        for k in range(LOOP_STEPS):
            emit(Step(LOOP_FIRST + k, i))
    for s in range(LOOP_FIRST + LOOPS * LOOP_STEPS, LAST_STEP + 1):
        emit(Step(s))


def cross_attention_kernel(nc, xT, x, cT, wqT, wkT, wvT, woT, bias_cols, bias_rows, ident,
                           minus_low, minus_high, out):
    ctx = ExitStack()
    with ctx:
        def sb(name, shape, dt, stack=ctx):
            return stack.enter_context(nc.sbuf_tensor(name, shape, dt))

        def sem(name):
            return ctx.enter_context(nc.semaphore(name))

        wq_h, wq_l = sb("wq_h", [P, KC, D], F32R), sb("wq_l", [P, KC, D], F32R)
        wo_h, wo_l = sb("wo_h", [P, KC, D], F32R), sb("wo_l", [P, KC, D], F32R)
        kT = sb("kT", [P, B, HALVES, 2, SKV], F32R)
        kblk = sb("kblk", [P, KSLOTS, HALVES, 2, WIDE], F32R)
        vblk_all = sb("vblk", [P, B * HALVES * NSEG * VP * VW], BF16)
        vblk = vblk_all[:].rearrange("p (b f n v w) -> p b f n v w", f=HALVES, n=NSEG, v=VP, w=VW)
        xT_raw = sb("xT_raw", [P, KC, PAIR], F32)
        xT_h, xT_l = sb("xT_h", [P, KC, PAIR], F32R), sb("xT_l", [P, KC, PAIR], F32R)
        q_low = [sb(f"q_low{n}", [P, HALVES, PAIR], F32R) for n in range(2)]
        q_high = [sb(f"q_high{n}", [P, HALVES, PAIR], F32R) for n in range(2)]
        q_lo = [sb(f"q_lo{n}", [P, HALVES, PAIR], F32R) for n in range(2)]
        ident_sb = sb("ident_sb", [P, P], F32)
        cols_sb = sb("cols_sb", [P, 3 * HALVES], F32)
        bq_sb, bk_sb, bv_sb = (cols_sb[:, HALVES * n:HALVES * (n + 1)] for n in range(3))
        rows_sb = sb("rows_sb", [P, 3 * D], F32)
        bo_sb, gamma_sb, beta_sb = (rows_sb[:, D * n:D * (n + 1)] for n in range(3))
        maxima = sb("maxima", [P, QT, MROWS], F32)
        shift, warm = sb("shift", [P, 1], F32), sb("warm", [P, 1], F32)
        recip = sb("recip", [P, HALVES, QT, HH], F32)
        stats_all = sb("stats", [P, 2, QT, 6], F32)
        meanvar_all = sb("meanvar", [P, 2, QT, 2], F32)
        rs_v_all, rs_t_all = sb("rs_v", [P, 2, QT], F32), sb("rs_t", [P, 2, QT], F32)
        rs_y = sb("rs_y", [P, 2, QT], F32)

        early = ExitStack()
        vparts = sb("vparts", [SKV, B, H, VP, VW], BF16, early)
        w_raw = sb("w_raw", [P, 4, KC, D], F32, early)
        wk_h, wk_l = sb("wk_h", [P, KC, D], F32R, early), sb("wk_l", [P, KC, D], F32R, early)
        wv_h, wv_l = sb("wv_h", [P, KC, D], F32R, early), sb("wv_l", [P, KC, D], F32R, early)
        c_raw = sb("c_raw", [P, 2, KC, GK], F32, early)
        c_h, c_l = sb("c_h", [P, 2, KC, GK], F32R, early), sb("c_l", [P, 2, KC, GK], F32R, early)
        vrest = sb("vrest", [SKV, 2, 2, D], F32, early)
        early.close()
        q_mix = [sb("q_mix0", [P, HALVES, 2, PAIR], F32R)]
        result = sb("result", [P, 2, QT, D], F32)
        y = sb("y", [P, QT, D], F32)
        used = 4 * (HALVES * 2 * PAIR + 2 * QT * D + QT * D)
        sb("unused", [P, (2 * B * H * VP * VW - used) // 4], F32)
        p32 = sb("p32", [P, P32SLOTS, 2, SQ], F32)
        p_h, p_l = sb("p_h", [P, PSLOTS, 2, SQ], FP16), sb("p_l", [P, PSLOTS, 2, SQ], FP16)
        ctx_n = sb("ctx_n", [P, QT, D], F32)
        ctx_h, ctx_l = sb("ctx_h", [P, HALVES, SQ], F32R), sb("ctx_l", [P, HALVES, SQ], F32R)
        x_rows = sb("x_rows", [P, 2, QT, D], F32)
        q_mix.append(sb("q_mix1", [P, HALVES, 2, PAIR], F32R))

        def bank(name, shape):
            return ctx.enter_context(nc.psum_tensor(name, shape, F32))

        ps_s = [bank(f"ps_s{n}", [P, 2, SQ]) for n in range(2)]
        ps_acc = [bank(f"ps_acc{n}", [P, 512]) for n in range(2)]
        ps_d = [bank(f"ps_d{n}", [P, 512]) for n in range(2)]
        ps_x = [bank(f"ps_x{n}", [P, 512]) for n in range(2)]

        ld_w = [sem(f"ld_w{n}") for n in range(4)]
        ld_c = [sem(f"ld_c{n}") for n in range(2)]
        ld_cols, ld_rows, ld_ident, ld_minus = sem("ld_cols"), sem("ld_rows"), sem("ld_ident"), sem("ld_minus")
        ld_xT = sem("ld_xT")
        ld_k = [sem(f"ld_k{n}") for n in range(2)]
        ld_twin = [sem(f"ld_twin{n}") for n in range(2)]
        ld_mix = [sem(f"ld_mix{n}") for n in range(2)]
        ld_v = [sem(f"ld_v{n}") for n in range(2)]
        ld_x = [sem(f"ld_x{n}") for n in range(2)]
        st_out = [sem(f"st_out{n}") for n in range(2)]
        st_last = sem("st_last")
        cleared_k = [sem(f"cleared_k{n}") for n in range(2)]
        cleared_v, cleared_parts, cleared_m = sem("cleared_v"), sem("cleared_parts"), sem("cleared_m")
        minus_set, minus_copied, shift_set = sem("minus_set"), sem("minus_copied"), sem("shift_set")
        w_hi, w_lo = sem("w_hi"), sem("w_lo")
        c_hi, c_lo = sem("c_hi"), sem("c_lo")
        bo_done = sem("bo_done")
        pe_bo, pe_k, pe_v = sem("pe_bo"), sem("pe_k"), sem("pe_v")
        k_hi, k_lo = sem("k_hi"), sem("k_lo")
        v_hi, v_rest1, v_mid, v_low = sem("v_hi"), sem("v_rest1"), sem("v_mid"), sem("v_low")
        x_hi, x_lo = sem("x_hi"), sem("x_lo")
        pe_q, q_hi, q_lo_done = sem("pe_q"), sem("q_hi"), sem("q_lo_done")
        pe_d, max_done, pe_m, m_done = sem("pe_d"), sem("max_done"), sem("pe_m"), sem("m_done")
        pe_s, exp16, rest16 = sem("pe_s"), sem("exp16"), sem("rest16")
        pe_e, rec_done, norm_done = sem("pe_e"), sem("rec_done"), sem("norm_done")
        pe_t, ctx_hi, ctx_lo = sem("pe_t"), sem("ctx_hi"), sem("ctx_lo")
        pe_o, x_biased, y_done = sem("pe_o"), sem("x_biased"), sem("y_done")
        stats_done, var_done = sem("stats_done"), sem("var_done")
        newton, newton_last = sem("newton"), sem("newton_last")
        centred, scaled, result_done, finished = sem("centred"), sem("scaled"), sem("result_done"), sem("finished")

        block = ctx.enter_context(nc.Block())

        xT_v = xT.rearrange("(k p) q -> p k q", p=P)
        cT_v = cT.rearrange("(k p) q -> p k q", p=P)
        x_v = x.rearrange("(b t p) d -> b p t d", p=P, t=QT)
        out_v = out.rearrange("(b t p) d -> b p t d", p=P, t=QT)
        WK, WV, WQ, WO = range(4)
        split_w = {WK: (wk_h, wk_l), WV: (wv_h, wv_l), WQ: (wq_h, wq_l), WO: (wo_h, wo_l)}
        V_TASKS = B // 2

        def merged(t):
            return (t + 1) * P <= MIX_LOW or t * P >= MIX_HIGH

        def context_turned(s, f):
            return (ps_d[0], 0) if s == B and f else (ps_x[0], f * SQ)

        low_rows, high_rows = slice(P - MROWS, P), slice(0, MROWS)
        low_cols, high_cols = LOW_TILES * P, PACKED - LOW_TILES * P
        v_batch = HALVES * NSEG * VP * VW
        stage = vblk_all[:, (B - 2) * v_batch:].bitcast(F32)
        stage_low = stage[low_rows, 0:HALVES * low_cols].rearrange("p (f c) -> p f c", f=HALVES)
        stage_high = stage[high_rows, 0:HALVES * high_cols].rearrange("p (f c) -> p f c", f=HALVES)

        @block.sync
        def _(sp):
            def load_weight(n, w):
                sp.dma_start(w_raw[:, n], w.rearrange("(k p) n -> p k n", p=P)).then_inc(ld_w[n], 16)

            def load_k(batch, slot):
                for h in range(HH):
                    rows = slice(DK * h, DK * (h + 1))
                    sp.dma_start(
                        kblk[rows, 2 * slot:2 * slot + 2, :, :, SKV * h:SKV * (h + 1)].rearrange("p b f l k -> p (b f l) k").bitcast(F32),
                        kT[rows, bass.ds(batch, 2)].rearrange("p b f l k -> p (b f l) k").bitcast(F32)).then_inc(ld_k[slot], 16)

            def load_twins(batch, slot):
                for h in range(HH):
                    rows, twin = slice(DK * h, DK * (h + 1)), slice((DK * h + P // 2) % P, (DK * h + P // 2) % P + DK)
                    k0, k1 = SKV * h, SKV * (h + 1)
                    k0, k1 = (k0, min(k1, MIX_LOW)) if h < HH // 2 else (max(k0, MIX_HIGH), k1)
                    sp.dma_start(kblk[twin, 2 * slot:2 * slot + 2, :, 0, k0:k1].rearrange("p b f k -> p (b f) k").bitcast(F32),
                                 kT[rows, bass.ds(batch, 2), :, 0, k0 - SKV * h:k1 - SKV * h]
                                 .rearrange("p b f k -> p (b f) k").bitcast(F32),
                                 allow_slow_non_contiguous=k1 - k0 == 1).then_inc(ld_twin[slot], 16)

            def load_mix(slot):
                low, high = slice(0, P // 2), slice(P // 2, P)
                for part, to, source, rows in ((0, low, q_low, low), (0, high, q_lo, low),
                                               (1, low, q_lo, high), (1, high, q_high, high)):
                    sp.dma_start(q_mix[slot][to, :, part].bitcast(F32), source[slot][rows].bitcast(F32)).then_inc(ld_mix[slot], 16)

            def load_v(part):
                sp.wait_ge(cleared_v, (1, 3)[part])
                for done in (v_hi, v_mid, v_low):
                    sp.wait_ge(done, V_TASKS // 2 * (part + 1))
                b0, b1 = HALVES * B // 2 * part, HALVES * B // 2 * (part + 1)
                src = vparts[:].rearrange("p b (f h) v w -> p (b f) h (v w)", h=HH)
                dst = vblk.rearrange("p b f n v w -> p (b f) n (v w)")
                for t, h, row, key, n, seg in SEGMENTS:
                    sp.dma_start(dst[row:row + n, b0:b1, seg], src[key:key + n, b0:b1, h]).then_inc(ld_v[part], 16)

            load_weight(WK, wkT)
            load_weight(WV, wvT)
            load_weight(WQ, wqT)
            sp.dma_start(xT_raw[:], xT_v[:, :, 0:PAIR]).then_inc(ld_xT, 16)
            sp.dma_start(stage_low, minus_low).then_inc(ld_minus, 16)
            sp.dma_start(stage_high, minus_high).then_inc(ld_minus, 16)
            sp.dma_start(ident_sb[:], ident).then_inc(ld_ident, 16)
            load_weight(WO, woT)
            sp.dma_start(rows_sb[:], bias_rows.partition_broadcast(P)).then_inc(ld_rows, 16)
            sp.wait_ge(cleared_k[0], 1)
            sp.wait_ge(cleared_k[1], 1)
            sp.wait_ge(k_lo, HALVES)
            load_k(0, 0)
            sp.wait_ge(x_lo, 1)
            sp.dma_start(xT_raw[:], xT_v[:, :, PAIR:2 * PAIR]).then_inc(ld_xT, 16)
            sp.wait_ge(cleared_k[1], 2)
            sp.wait_ge(minus_set, 2)
            for slot in range(1, KSLOTS):
                for rows, c0, c1 in ((low_rows, 0, low_cols), (high_rows, low_cols, PACKED)):
                    sp.dma_start(kblk[rows, slot, :, 1, c0:c1].bitcast(F32),
                                 kblk[rows, 0, :, 1, c0:c1].bitcast(F32)).then_inc(minus_copied, 16)
            load_k(2, 1)
            load_v(0)

            def step(S):
                s = S.first
                if S.load_x:
                    S.wait(sp, x_lo, 1, 4, by=2)
                    sp.dma_start(xT_raw[:], xT_v[:, :, bass.ds(S.lin(SQ, 4 * SQ), PAIR)]).then_inc(ld_xT, 16)
                if S.load_k:
                    if s == 2:
                        sp.wait_ge(k_lo, HALVES * GROUPS)
                    S.wait(sp, pe_s, UNITS, 0)
                    load_k(S.lin(1, 2), (s // 2 + 1) % 2)
                    load_twins(S.lin(1, 2), (s // 2 + 1) % 2)
                if S.scores:
                    if s == 0:
                        sp.wait_ge(pe_v, V_TASKS)
                        sp.wait_ge(pe_bo, 1)
                    S.wait(sp, y_done, 1, -1)
                    sp.dma_start(x_rows[:, s % 2], S.batch(x_v, 0, 0)).then_inc(ld_x[s % 2], 16)
                if s == 0:
                    load_twins(2, 1)
                if s == 1:
                    load_v(1)
                if S.store:
                    if s < LAST_STEP:
                        S.wait(sp, result_done, 1, -2)
                        sp.dma_start(S.batch(out_v, 3, 0), result[:, (s - 3) % 2]).then_inc(st_out[(s - 3) % 2], 16)
                    else:
                        for t in range(QT):
                            sp.wait_ge(finished, t + 1)
                            sp.dma_start(out_v[B - 1][:, t], result[:, (B - 1) % 2, t]).then_inc(st_last, 16)
                if S.project_q:
                    S.wait(sp, q_lo_done, 1, 4)
                    if s == 2:
                        sp.wait_ge(ld_v[1], 16 * NSEG)
                    load_mix((s // 2 + 1) % 2)

            all_steps(sp, step)
            sp.wait_ge(st_out[0], 16 * B // 2)
            sp.wait_ge(st_out[1], 16 * (B // 2 - 1))
            sp.wait_ge(st_last, 16 * QT)

        @block.tensor
        def _(pe):
            def mm(o, w, m, start, stop):
                return nc.tensor.matmul(o, w, m, start=start, stop=stop, skip_group_check=True)

            def three(o, w, m):
                for k in range(KC):
                    ins = chunk(o, w, m, k, k == 0)
                return ins

            def chunk(o, w, m, k, start):
                for a, b in ((0, 0), (0, 1), (1, 0)):
                    ins = mm(o, w(a, k), m(b, k), start and (a, b) == (0, 0), k == KC - 1 and (a, b) == (1, 0))
                return ins

            def project_k(g):
                if g:
                    pe.wait_ge(c_lo, g + 1)
                for f in range(HALVES):
                    if g == 0 and f == 0:
                        for i, (a, b) in enumerate(((0, 0), (1, 0), (0, 1))):
                            if i == 0:
                                pe.wait_ge(w_hi, 1)
                                pe.wait_ge(c_hi, 1)
                            elif i == 1:
                                pe.wait_ge(w_lo, 1)
                            else:
                                pe.wait_ge(c_lo, 1)
                            for k in range(KC):
                                ins = mm(ps_x[0][:, 0:GK], (wk_h, wk_l)[a][:, k, 0:P], (c_h, c_l)[b][:, 0, k, :],
                                         (i, k) == (0, 0), (i, k) == (2, KC - 1))
                        ins.then_inc(pe_k, 1)
                        continue
                    if g == 2:
                        pe.wait_ge(q_lo_done, f + 1)
                    elif g:
                        pe.wait_ge(k_lo, HALVES * (g - 1) + f + 1)
                    three(ps_x[f][:, 0:GK], lambda a, k: (wk_h, wk_l)[a][:, k, f * P:(f + 1) * P],
                          lambda b, k: (c_h, c_l)[b][:, g % 2, k, :]).then_inc(pe_k, 1)

            def project_v(g, n):
                if g:
                    pe.wait_ge(v_rest1, 2 * g + n - 1)
                for j in range(2):
                    at = (2 * n + j) * SKV
                    ins = three(ps_acc[n][0:SKV, j * D:(j + 1) * D],
                                lambda a, k: (c_h, c_l)[a][:, g % 2, k, at:at + SKV],
                                lambda b, k: (wv_h, wv_l)[b][:, k, :])
                ins.then_inc(pe_v, 1)

            def project_q(f):
                three(ps_x[f][:], lambda a, k: (wq_h, wq_l)[a][:, k, f * P:(f + 1) * P],
                      lambda b, k: (xT_h, xT_l)[b][:, k, :]).then_inc(pe_q, 1)

            project_k(0)
            pe.wait_ge(w_lo, 2)
            project_v(0, 0)
            project_v(0, 1)
            project_k(1)
            project_v(1, 0)
            pe.wait_ge(w_lo, 3)
            pe.wait_ge(x_lo, 1)
            for f in range(HALVES):
                pe.wait_ge(k_lo, HALVES + f + 1)
                project_q(f)

            def step(S, between={}):
                s = S.first
                nb = s + 1

                def max_bank(j):
                    return ps_d[((DMAX + 1) * nb + j) % 2]

                def max_scores(j):
                    t, f, n = j // 4, j // 2 % 2, j % 2
                    rows = slice(n * P // 2, (n + 1) * P // 2)
                    if j == 0:
                        if nb % 2 == 0:
                            S.wait(pe, ld_k[nb // 2 % 2], 16 * HH, 16 * HH * (5 - nb % 4), by=4)
                            S.wait(pe, q_hi, 1, 3)
                        S.wait(pe, max_done, DMAX, DMAX)
                    elif j == 1:
                        S.wait(pe, m_done, 1, 1)
                    else:
                        S.wait(pe, max_done, DMAX, DMAX + j - 1)
                    q0 = nb % 2 * SQ + t * P
                    mm(max_bank(j)[:, 0:DMAX_HEADS * SKV], q_low[nb // 2 % 2][rows, f, q0:q0 + P],
                       kblk[rows, nb % KSLOTS, f, 0, n * DMAX_HEADS * SKV:(n + 1) * DMAX_HEADS * SKV],
                       True, True).then_inc(pe_d, 1)

                def turn_maxima():
                    S.wait(pe, max_done, DMAX, 2 * DMAX)
                    for t in range(QT):
                        ins = nc.tensor.transpose(max_bank(DMAX)[0:MROWS, t * P:(t + 1) * P], maxima[:, t, :], ident_sb[:])
                    ins.then_inc(pe_m, 1)

                def score_tile(u, n):
                    f, t = divmod(2 * u + n, TILES)
                    if n == 0:
                        S.wait(pe, exp16, UNITS, u - 1)
                        if s == 0 and u == 1:
                            pe.wait_ge(bo_done, 1)
                    if u == 0 and n == 0:
                        S.wait(pe, m_done, 1, 1)
                        S.wait(pe, q_lo_done, 1, 2 - s % 2)
                        if s == 0:
                            pe.wait_ge(minus_copied, 2 * (KSLOTS - 1) * 16)
                        elif s % 2 == 0:
                            S.wait(pe, ld_twin[s // 2 % 2], 16 * HH, 16 * HH * (s % 4), by=4)
                            S.wait(pe, ld_mix[s // 2 % 2], 16 * 4, 16 * 4 * (s % 4), by=4)
                    tile = slice(t * P, (t + 1) * P)
                    cols = slice(s % 2 * SQ, (s % 2 + 1) * SQ)
                    slot = s // 2 % 2
                    q = (q_low if t < LOW_TILES else q_high)[slot][:, f, cols]
                    o = ps_s[(UNITS * s + u) % 2][:, n, :]
                    if s >= 2 and merged(t):
                        mm(o, kblk[:, s % KSLOTS, f, 0, tile], q_mix[slot][:, f, t >= LOW_TILES, cols], True, False)
                    else:
                        mm(o, kblk[:, s % KSLOTS, f, 0, tile], q, True, False)
                        mm(o, kblk[:, s % KSLOTS, f, 0, tile], q_lo[slot][:, f, cols], False, False)
                    ins = mm(o, kblk[:, s % KSLOTS, f, 1, tile], q, False, True)
                    if n == 1:
                        ins.then_inc(pe_s, 1)

                def weigh(u, n, back):
                    g = 2 * u + n
                    f, t = divmod(g, TILES)
                    slot = (UNITS * (s - back) + u) % PSLOTS
                    heads = [x[1] for x in SEGMENTS if x[0] == t]
                    s0 = [x[5] for x in SEGMENTS if x[0] == t][0]
                    if n == 0:
                        S.wait(pe, rest16, UNITS, u + 1 - UNITS * back)
                    if t == 0:
                        S.wait(pe, norm_done, HALVES, f + 1 - HALVES * (back + 1))
                    if g == 0:
                        if s == LOOP_FIRST - 1:
                            pe.wait_ge(ld_v[1], 16 * NSEG)
                        if s == 0:
                            pe.wait_ge(ld_v[0], 16 * NSEG)
                            pe.wait_ge(v_rest1, V_TASKS)
                    for qt in range(QT):
                        at = (qt * HH + heads[0]) * VW
                        o = ps_acc[f][:, at:at + len(heads) * VW].rearrange("p (n w) -> p n w", w=VW)
                        for j, (p, v) in enumerate(((p_h, 0), (p_h, 1), (p_h, 2), (p_l, 0), (p_l, 1))):
                            ins = mm(o, p[:, slot, n, qt * P:(qt + 1) * P],
                                     S.batch(vblk, back, 1)[:, f, s0:s0 + len(heads), v, :],
                                     t == 0 and qt == 0 and j == 0, t == TILES - 1 and qt == QT - 1 and j == 4)
                    if n == 1:
                        ins.then_inc(pe_e, 1)

                def turn_context(*halves):
                    S.wait(pe, norm_done, HALVES, halves[-1] - 1)
                    if S.project_q:
                        S.wait(pe, q_lo_done, 1, 3)
                    else:
                        S.wait(pe, ctx_lo, 1, -1)
                    for f in halves:
                        bank, at = context_turned(s, f)
                        for qt in range(QT):
                            ins = nc.tensor.transpose(bank[:, at + qt * P:at + (qt + 1) * P],
                                                      ctx_n[:, qt, f * P:(f + 1) * P], ident_sb[:])
                    ins.then_inc(pe_t, 1)

                def project_out(*halves):
                    S.wait(pe, ctx_lo, 1, halves[-1] if s == B else 0)
                    if S.project_q:
                        S.wait(pe, q_lo_done, 1, 4)
                    else:
                        S.wait(pe, y_done, 1, -1)
                    if s == 1:
                        pe.wait_ge(w_lo, 4)
                    for qt in range(QT):
                        for k in halves:
                            ins = chunk(ps_x[1][:, qt * D:(qt + 1) * D],
                                        lambda a, k: (ctx_h, ctx_l)[a][:, k, qt * P:(qt + 1) * P],
                                        lambda b, k: (wo_h, wo_l)[b][:, k, :], k,
                                        k == 0 and (qt == 0 or len(halves) == HALVES))
                    if HALVES - 1 in halves:
                        ins.then_inc(pe_o, 1)

                def next_q(f):
                    if s == 0:
                        pe.wait_ge(k_lo, HALVES * (GROUPS - 1) + f + 1)
                    if f == 0:
                        S.wait(pe, x_lo, 1, 4, by=2)
                        S.wait(pe, ctx_lo, 1, -1)
                    else:
                        S.wait(pe, y_done, 1, -1)
                    project_q(f)

                tasks = {(0, 0): 0, (0, 1): 1, (1, 0): 2, (1, 1): 3, (2, 0): 4, (2, 1): 5, (3, 0): 6, (3, 1): 7,
                         (4, 1): DMAX}
                if S.project_q and s > 0:
                    tasks = {(0, 0): 0, (0, 1): 1, (0, 2): 2, (1, 0): 3, (1, 2): 4, (2, 0): 5, (2, 2): 6, (3, 1): 7,
                             (4, 1): DMAX}
                for u in range(UNITS):
                    for part in range(4):
                        if part < 2 and S.scores:
                            score_tile(u, part)
                        if part >= 2 and u < 2 and S.output:
                            weigh(u + 3, part - 2, 1)
                        if part >= 2 and u >= 2 and S.scores:
                            weigh(u - 2, part - 2, 0)
                        if (u, part) == (3, 1) and S.output and s < B:
                            turn_context(0, 1)
                        if (u, part) in tasks and S.maxima:
                            j = tasks[u, part]
                            max_scores(j) if j < DMAX else turn_maxima()
                        if part == 1 and u < 2 and S.project_q:
                            next_q(u)
                    if u == 4 and S.output and s < B:
                        project_out(0, 1)
                    if u in between:
                        between[u]()
                if s == B:
                    for stage in (turn_context, project_out):
                        for f in range(HALVES):
                            stage(f)

            def project_bias():
                for k in range(KC):
                    ins = mm(ps_s[1][:, 0, :], bv_sb[:, k:k + 1].to_broadcast([P, P]), w_raw[:, WO, k, :], k == 0, k == KC - 1)
                ins.then_inc(pe_bo, 1)

            pe.wait_ge(cleared_m, 1)
            pe.wait_ge(ld_ident, 16)
            pe.wait_ge(ld_cols, 16)
            pe.wait_ge(ld_w[WO], 16)
            project_v(1, 1)
            def bias_and_key():
                project_bias()
                project_k(2)

            step(Step(-1), {0: bias_and_key, 1: lambda: project_v(2, 0), 2: lambda: project_v(2, 1),
                            3: lambda: project_k(3)})
            project_v(3, 0)
            project_v(3, 1)
            all_steps(pe, step)

        @block.scalar
        def _(act):
            copy, add = ACT.Copy, ACT.Identity
            weights = list(split_w.items())

            def load_context(g):
                act.dma_start(c_raw[:, g % 2], cT_v[:, :, g * GK:(g + 1) * GK]).then_inc(ld_c[g % 2], 16)

            load_context(0)
            act.wait_ge(shift_set, 1)
            nc.scalar.activation(warm[:], shift[:], ACT.Exp)
            act.dma_start(cols_sb[:], bias_cols).then_inc(ld_cols, 16)
            load_context(1)

            def weight_hi(n):
                w, (hi, _) = weights[n]
                act.wait_ge(ld_w[w], 16)
                nc.scalar.activation(hi[:], w_raw[:, w], copy).then_inc(w_hi, 1)

            def context_hi(g):
                act.wait_ge(ld_c[g % 2], 16 * (g // 2 + 1))
                if g >= 2:
                    act.wait_ge(pe_v, 2 * (g - 1))
                nc.scalar.activation(c_h[:, g % 2], c_raw[:, g % 2], copy).then_inc(c_hi, 1)

            def key_hi(g):
                for f in range(HALVES):
                    act.wait_ge(pe_k, HALVES * g + f + 1)
                    nc.scalar.activation(kT[:, GROUP * g:GROUP * (g + 1), f, 0, :],
                                         ps_x[f][:, 0:GK].rearrange("p (b k) -> p b k", k=SKV), add,
                                         bias=bk_sb[:, f:f + 1]).then_inc(k_hi, 1)

            def value_part(v, part):
                return vparts[:, 2 * v:2 * v + 2, :, part, 0:DK].rearrange("p b h w -> p (b h) w")

            def value_hi(v):
                act.wait_ge(pe_v, v + 1)
                nc.scalar.activation(value_part(v, 0), ps_acc[v % 2][0:SKV, :].rearrange("p (n w) -> p n w", w=DK),
                                     copy).then_inc(v_hi, 1)

            def value_mid(v):
                act.wait_ge(v_rest1, v + 1)
                nc.scalar.activation(value_part(v, 1), vrest[:, v % 2].rearrange("p b (h w) -> p (b h) w", w=DK),
                                     copy).then_inc(v_mid, 1)

            def query_hi(f, slot):
                nc.scalar.activation(q_low[slot][:, f], ps_x[f][:], add, bias=bq_sb[:, f:f + 1])
                nc.scalar.activation(q_high[slot][:, f], ps_x[f][:], add, bias=bq_sb[:, f:f + 1]).then_inc(q_hi, 1)

            def split_x():
                nc.scalar.activation(xT_h[:], xT_raw[:], copy).then_inc(x_hi, 1)

            weight_hi(0)
            context_hi(0)
            weight_hi(1)
            act.wait_ge(ld_cols, 16)
            key_hi(0)
            context_hi(1)
            act.wait_ge(c_lo, 1)
            load_context(2)
            weight_hi(2)
            value_hi(0)
            act.wait_ge(ld_xT, 16)
            split_x()
            value_hi(1)
            key_hi(1)
            value_mid(0)
            value_mid(1)
            value_hi(2)
            context_hi(2)
            for f in range(HALVES):
                act.wait_ge(pe_q, f + 1)
                query_hi(f, 0)

            def step(S):
                s = S.first

                def exponentials(u):
                    S.wait(act, pe_s, UNITS, u + 1)
                    S.wait(act, rest16, UNITS, u + 1 - P32SLOTS)
                    S.wait(act, pe_e, UNITS, u + 1 - PSLOTS)
                    if s == 0 and u == 0:
                        act.wait_ge(pe_bo, 1)
                        act.wait_ge(w_lo, 4)
                    n = UNITS * s + u
                    nc.scalar.activation(p32[:, n % P32SLOTS], ps_s[n % 2][:], ACT.Exp, scale=SCALE)
                    nc.scalar.activation(p_h[:, n % PSLOTS], ps_s[n % 2][:], ACT.Exp, scale=SCALE).then_inc(exp16, 1)

                def context_hi_part(*halves):
                    f, n = halves[0], len(halves)
                    S.wait(act, pe_t, 1, f if s == B else 0)
                    S.wait(act, pe_o, 1, -1)
                    bank, at = context_turned(s, f)
                    nc.scalar.activation(ctx_h[:, f:f + n], bank[:, at:at + n * SQ].rearrange("p (f q) -> p f q", q=SQ),
                                         copy).then_inc(ctx_hi, 1)

                def write_maxima():
                    S.wait(act, pe_m, 1, 2)
                    if s == -1:
                        act.wait_ge(shift_set, 1)
                    nb = s + 1
                    cols = slice(nb % 2 * SQ, (nb % 2 + 1) * SQ)
                    m = ps_d[((DMAX + 1) * nb + DMAX) % 2][0:MROWS, 0:SQ].unsqueeze(1).broadcast_to([MROWS, HALVES, SQ])
                    nc.scalar.activation(q_low[nb // 2 % 2][low_rows, :, cols], m, add, bias=shift[low_rows, 0:1])
                    nc.scalar.activation(q_high[nb // 2 % 2][high_rows, :, cols], m, add,
                                         bias=shift[high_rows, 0:1]).then_inc(m_done, 1)

                for u in range(UNITS):
                    if u == 4 and S.maxima:
                        write_maxima()
                    if u == 3 and S.output and s < B and S.project_q:
                        context_hi_part(0, 1)
                    if S.scores:
                        exponentials(u)
                    if s == 0 and u < 2:
                        value_mid(V_TASKS - 2 + u)
                    if u < HALVES and S.project_q:
                        S.wait(act, pe_q, 1, 3 + u)
                        S.wait(act, pe_s, UNITS, 0)
                        query_hi(u, (s // 2 + 1) % 2)
                    if u == (2 if S.project_q else 1) and S.store and s < LAST_STEP:
                        S.wait(act, newton, CHAIN, -2 * CHAIN)
                        S.wait(act, centred, QT, -2 * QT)
                        for t in range(QT):
                            r = result[:, (s - 3) % 2, t]
                            nc.scalar.activation(r, r, copy, scale=rs_y[:, (s - 3) % 2, t:t + 1]).then_inc(scaled, 1)
                    if s == B and u == 0:
                        context_hi_part(0)
                        context_hi_part(1)
                    if u == 3 and S.output and s < B and not S.project_q:
                        context_hi_part(0, 1)
                    if u == 3 and S.split_x:
                        S.wait(act, ld_xT, 8, 8 * 5)
                        S.wait(act, pe_q, 1, 3)
                        split_x()

            act.wait_ge(c_lo, 2)
            load_context(3)
            act.wait_ge(ld_xT, 32)
            act.wait_ge(pe_q, HALVES)
            split_x()
            value_mid(2)
            value_hi(3)
            context_hi(3)
            key_hi(2)
            weight_hi(3)
            value_mid(3)
            value_hi(4)
            value_hi(5)
            key_hi(3)
            value_mid(4)
            value_mid(5)
            step(Step(-1))
            value_hi(6)
            value_hi(7)
            all_steps(act, step)

        @block.vector
        def _(dve):
            weights = list(split_w.items())
            v_ = nc.vector

            def lo(out_, whole, hi):
                return v_.tensor_tensor(out_, whole, hi.bitcast(F32), ALU.subtract)

            def lo_biased(out_, whole, bias, hi):
                return v_.scalar_tensor_tensor(out_, whole, bias, hi.bitcast(F32), ALU.add, ALU.subtract)

            v_.memset(shift[:], -EXP_SHIFT / SCALE).then_inc(shift_set, 1)
            v_.memset(kblk[:, 0].bitcast(F32), 0.0).then_inc(cleared_k[0], 1)
            v_.memset(maxima[:], 0.0).then_inc(cleared_m, 1)

            def weight_lo(n):
                w, (hi, low) = weights[n]
                dve.wait_ge(w_hi, n + 1)
                lo(low[:], w_raw[:, w], hi[:]).then_inc(w_lo, 1)

            def context_lo(g):
                dve.wait_ge(c_hi, g + 1)
                lo(c_l[:, g % 2], c_raw[:, g % 2], c_h[:, g % 2]).then_inc(c_lo, 1)

            def key_lo(g):
                for f in range(HALVES):
                    dve.wait_ge(k_hi, HALVES * g + f + 1)
                    part = kT[:, GROUP * g:GROUP * (g + 1), f]
                    lo_biased(part[:, :, 1, :], ps_x[f][:, 0:GK].rearrange("p (b k) -> p b k", k=SKV),
                              bk_sb[:, f:f + 1], part[:, :, 0, :]).then_inc(k_lo, 1)

            def value_part(v, part):
                return vparts[:, 2 * v:2 * v + 2, :, part, 0:DK].rearrange("p b h w -> p (b h) w")

            def value_rest(v):
                dve.wait_ge(v_hi, v + 1)
                if v >= 2:
                    dve.wait_ge(v_low, v - 1)
                v_.tensor_tensor(vrest[:, v % 2].rearrange("p b (h w) -> p (b h) w", w=DK),
                                 ps_acc[v % 2][0:SKV, :].rearrange("p (n w) -> p n w", w=DK),
                                 value_part(v, 0), ALU.subtract).then_inc(v_rest1, 1)

            def query_lo(f, slot):
                lo_biased(q_lo[slot][:, f], ps_x[f][:], bq_sb[:, f:f + 1], q_high[slot][:, f]).then_inc(q_lo_done, 1)

            def split_x():
                lo(xT_l[:], xT_raw[:], xT_h[:]).then_inc(x_lo, 1)

            def set_minus():
                dve.wait_ge(cleared_k[0], 1)
                dve.wait_ge(ld_minus, 32)
                v_.tensor_copy(kblk[low_rows, 0, :, 1, 0:low_cols], stage_low).then_inc(minus_set, 1)
                v_.tensor_copy(kblk[high_rows, 0, :, 1, low_cols:PACKED], stage_high).then_inc(minus_set, 1)

            weight_lo(0)
            context_lo(0)
            weight_lo(1)
            dve.wait_ge(ld_cols, 16)
            key_lo(0)
            context_lo(1)
            weight_lo(2)
            value_rest(0)
            dve.wait_ge(x_hi, 1)
            split_x()
            value_rest(1)
            key_lo(1)
            set_minus()
            value_rest(2)
            context_lo(2)
            for f in range(HALVES):
                dve.wait_ge(q_hi, f + 1)
                query_lo(f, 0)

            def step(S, between={}):
                s = S.first
                last = s == B + 1
                own = int(last)
                stats, meanvar = stats_all[:, own], meanvar_all[:, own]
                rs_v, rs_t = rs_v_all[:, own], rs_t_all[:, own]
                y_s = x_rows[:, (B - 1) % 2] if last else y[:]

                def accumulated(f):
                    return ps_acc[f][:, 0:QT * HH * VW].rearrange("p (t h w) -> p t h w", t=QT, w=VW)

                def max_of(j):
                    t, f, n = j // 4, j // 2 % 2, j % 2
                    S.wait(dve, pe_d, DMAX, DMAX + j + 1)
                    if j == 0:
                        S.wait(dve, pe_m, 1, 1)
                    h0 = f * HH + n * DMAX_HEADS
                    v_.tensor_reduce(maxima[:, t, h0:h0 + DMAX_HEADS],
                                     ps_d[((DMAX + 1) * (s + 1) + j) % 2][:, 0:DMAX_HEADS * SKV]
                                     .rearrange("p (h k) -> p h k", k=SKV), AX.X, ALU.max).then_inc(max_done, 1)
                    if j in between:
                        between[j]()

                def denominators(f):
                    S.wait(dve, pe_e, UNITS, 0 if f else UNITS // 2 + 1 - UNITS)
                    v_.reciprocal(recip[:, f], accumulated(f)[:, :, :, DK]).then_inc(rec_done, 1)

                def normalize(f):
                    S.wait(dve, rec_done, HALVES, f + 1 - HALVES)
                    if f == 0:
                        S.wait(dve, pe_t, 1, -1)
                    v_.tensor_tensor(ctx_n[:, :, f * P:(f + 1) * P].rearrange("p t (h w) -> p t h w", w=DK),
                                     accumulated(f)[:, :, :, 0:DK],
                                     recip[:, f].unsqueeze(3).broadcast_to([P, QT, HH, DK]),
                                     ALU.mult).then_inc(norm_done, 1)

                def bias_x():
                    slot = (s - 1) % 2
                    S.wait(dve, ld_x[slot], 8, 8 - 8 * slot)
                    v_.tensor_tensor(x_rows[:, slot], x_rows[:, slot], bo_sb.unsqueeze(1).broadcast_to([P, QT, D]),
                                     ALU.add).then_inc(x_biased, 1)

                def residual():
                    if s == 2:
                        dve.wait_ge(ld_v[1], 16 * NSEG)
                    S.wait(dve, pe_o, 1, -1)
                    S.wait(dve, x_biased, 1, -1)
                    if not last:
                        S.wait(dve, centred, QT, -2 * QT)
                    v_.tensor_tensor(y_s.rearrange("p t d -> p (t d)"), ps_x[1][:],
                                     x_rows[:, s % 2].rearrange("p t d -> p (t d)"), ALU.add).then_inc(y_done, 1)

                def statistics(t):
                    v_.bn_stats(stats[:, t], y_s[:, t]).then_inc(stats_done, 1)

                def aggregate():
                    for t in range(QT):
                        v_.bn_aggr(meanvar[:, t], stats[:, t]).then_inc(var_done, 1)

                def chain(n, root, rs_v, rs_t, variance):
                    guess = [
                        lambda: v_.tensor_scalar(rs_v, variance, LN_EPS, None, ALU.add),
                        lambda: v_.tensor_scalar(rs_t.bitcast(I32), rs_v.bitcast(I32), 1, None,
                                                 ALU.logical_shift_right),
                        lambda: v_.tensor_scalar(root.bitcast(I32), rs_t.bitcast(I32), -1.0, float(0x5F3759DF),
                                                 ALU.mult, ALU.add)]
                    newton_step = [
                        lambda: v_.scalar_tensor_tensor(rs_t, root, -0.5, root, ALU.mult, ALU.mult),
                        lambda: v_.tensor_tensor(rs_t, rs_t, rs_v, ALU.mult),
                        lambda: v_.scalar_tensor_tensor(root, rs_t, 1.5, root, ALU.add, ALU.mult)]
                    return (guess + NEWTON * newton_step)[n]()

                root = rs_y[:, s % 2]

                def small(n):
                    if n == 0:
                        S.wait(dve, var_done, QT, -QT)
                    else:
                        S.wait(dve, newton, CHAIN, n - 2 * CHAIN)
                    if n == 2:
                        S.wait(dve, scaled, QT, -3 * QT)
                    chain(n, root, rs_v, rs_t, meanvar[:, :, 1]).then_inc(newton, 1)

                def small_before(n):
                    dve.wait_ge(newton, CHAIN * (B - 2) + n)
                    chain(n, rs_y[:, (B - 2) % 2], rs_v_all[:, 0], rs_t_all[:, 0],
                          meanvar_all[:, 0, :, 1]).then_inc(newton, 1)

                def small_last(n):
                    if n == 0:
                        dve.wait_ge(var_done, QT * B)
                    else:
                        dve.wait_ge(newton_last, n)
                    if n == 2:
                        dve.wait_ge(scaled, QT * (B - 2))
                    chain(n, root, rs_v, rs_t, meanvar[:, :, 1]).then_inc(newton_last, 1)

                def centre_before(t):
                    o = (B - 2) % 2
                    if t == 0:
                        dve.wait_ge(st_out[o], 16 * (B - 2) // 2)
                    v_.scalar_tensor_tensor(result[:, o, t], y[:, t], meanvar_all[:, 0, t, 0:1], gamma_sb,
                                            ALU.subtract, ALU.mult).then_inc(centred, 1)

                def centre(t):
                    o = s % 2
                    if t == 0:
                        S.wait(dve, st_out[o], 8, -16 - 8 * o)
                    v_.scalar_tensor_tensor(result[:, o, t], y_s[:, t], meanvar[:, t, 0:1], gamma_sb,
                                            ALU.subtract, ALU.mult).then_inc(centred, 1)

                def context_lo_part(*halves):
                    f, n = halves[0], len(halves)
                    S.wait(dve, ctx_hi, 1, f if s == B else 0)
                    S.wait(dve, pe_o, 1, -1)
                    bank, at = context_turned(s, f)
                    lo(ctx_l[:, f:f + n], bank[:, at:at + n * SQ].rearrange("p (f q) -> p f q", q=SQ),
                       ctx_h[:, f:f + n]).then_inc(ctx_lo, 1)

                def queries(f):
                    S.wait(dve, q_hi, 1, 3 + f)
                    query_lo(f, (s // 2 + 1) % 2)

                def when(on, *what):
                    if on:
                        for fn, *args in what:
                            fn(*args)

                if last:
                    residual()
                    small_before(3)
                    dve.wait_ge(y_done, B)
                    statistics(0)
                    statistics(1)
                    small_before(4)
                    centre_before(0)
                    dve.wait_ge(stats_done, QT * B)
                    small_before(5)
                    aggregate()
                    small_before(6)
                    for n in range(CHAIN):
                        small_last(n)
                        if n + 7 < CHAIN:
                            small_before(n + 7)
                        if n == 1:
                            centre_before(1)
                        if n in (6, 8):
                            centre((n - 6) // 2)
                    dve.wait_ge(newton_last, CHAIN)
                    for t in range(QT):
                        r = result[:, (B - 1) % 2, t]
                        v_.scalar_tensor_tensor(r, r, root[:, t:t + 1], beta_sb, ALU.mult, ALU.add).then_inc(finished, 1)
                    return

                when(S.output, (denominators, 0))
                when(S.maxima, (max_of, 0))
                when(S.output, (normalize, 0))
                when(S.maxima, (max_of, 1))
                when(s == B, (denominators, 1), (normalize, 1))
                when(S.norm, (residual,))
                when(s == B, (context_lo_part, 0))
                when(S.maxima, (max_of, 2))
                if S.norm:
                    S.wait(dve, y_done, 1, -1)
                when(S.maxima, (max_of, 3))
                when(S.norm, (statistics, 0))
                when(S.project_q, (queries, 0))
                when(s == B, (context_lo_part, 1))
                when(S.norm, (statistics, 1))
                when(S.output and s < B, (denominators, 1))
                when(s == B - 1, (bias_x,))
                if S.norm:
                    S.wait(dve, stats_done, QT, -QT)
                when(S.maxima, (max_of, 4))
                when(S.norm, (aggregate,))
                when(S.project_q, (max_of, 5))
                when(S.output and s < B, (normalize, 1))
                when(S.norm, (small, 0))
                when(S.project_q, (queries, 1))
                when(S.maxima and not S.project_q, (max_of, 5))
                when(S.norm, (small, 1))
                when(S.maxima, (max_of, 6))
                when(S.norm, (small, 2))
                if s == B:
                    return
                when(S.maxima, (max_of, 7))
                when(S.norm, (small, 3))
                when(S.output and s < B, (context_lo_part, 0, 1))
                when(S.norm, (small, 4), (centre, 0), (small, 5), (centre, 1), (small, 6))
                if S.split_x:
                    S.wait(dve, x_hi, 1, 5, by=2)
                    split_x()
                when(S.norm, *((small, n) for n in range(7, CHAIN)))

            def values(g):
                value_rest(2 * g)
                value_rest(2 * g + 1)

            def output_bias():
                dve.wait_ge(ld_rows, 16)
                dve.wait_ge(pe_bo, 1)
                v_.tensor_tensor(bo_sb, ps_s[1][:, 0, :], bo_sb, ALU.add).then_inc(bo_done, 1)

            def split_second_x():
                dve.wait_ge(x_hi, 2)
                split_x()

            step(Step(-1), {1: split_second_x, 3: lambda: (value_rest(3), context_lo(3)), 5: lambda: key_lo(2)})
            values(2)
            key_lo(3)
            weight_lo(3)
            output_bias()
            values(3)
            all_steps(dve, step)

        @block.gpsimd
        def _(pool):
            g_ = nc.gpsimd
            g_.memset(kblk[:, 1].bitcast(F32), 0.0).then_inc(cleared_k[1], 1)
            g_.memset(kblk[:, 2:KSLOTS].bitcast(F32), 0.0).then_inc(cleared_k[1], 1)
            g_.memset(vparts[:, :, :, 0, DK:VW], 1.0).then_inc(cleared_parts, 1)
            g_.memset(vparts[:, :, :, 1:VP, DK:VW], 0.0).then_inc(cleared_parts, 1)
            words = vblk_all[:].bitcast(U32)
            staged = (B - 2) * v_batch // 2

            def value_low(v):
                pool.wait_ge(v_mid, v + 1)
                g_.tensor_tensor(vparts[:, 2 * v:2 * v + 2, :, 2, 0:DK].rearrange("p b h w -> p (b h) w"),
                                 vrest[:, v % 2].rearrange("p b (h w) -> p (b h) w", w=DK),
                                 vparts[:, 2 * v:2 * v + 2, :, 1, 0:DK].rearrange("p b h w -> p (b h) w"),
                                 ALU.subtract).then_inc(v_low, 1)

            half = B // 2 * v_batch // 2
            g_.memset(words[:, 0:half], 0).then_inc(cleared_v, 1)
            for v in range(3):
                value_low(v)
            g_.memset(words[:, half:staged], 0).then_inc(cleared_v, 1)
            value_low(3)
            pool.wait_ge(minus_set, 2)
            g_.memset(words[:, staged:], 0).then_inc(cleared_v, 1)
            for v in range(4, V_TASKS - 2):
                value_low(v)

            def step(S):
                s = S.first
                for u in range(UNITS):
                    if S.scores:
                        n = UNITS * s + u
                        S.wait(pool, exp16, UNITS, u + 1)
                        if s == 0 and u == 0:
                            pool.wait_ge(pe_k, HALVES * GROUPS)
                        g_.tensor_tensor(p_l[:, n % PSLOTS], p32[:, n % P32SLOTS], p_h[:, n % PSLOTS],
                                         ALU.subtract).then_inc(rest16, 1)
                    if s == 0 and u in (2, 3):
                        value_low(V_TASKS - 4 + u)
                    if u == (2 if s < B - 1 else 4) and S.store and s < LAST_STEP:
                        r = result[:, (s - 3) % 2]
                        S.wait(pool, scaled, QT, -2 * QT)
                        g_.tensor_tensor(r, r, beta_sb.unsqueeze(1).broadcast_to([P, QT, D]),
                                         ALU.add).then_inc(result_done, 1)
                    if u == 3 and S.output and s != B - 1:
                        slot = (s - 1) % 2
                        xr = x_rows[:, slot]
                        S.wait(pool, ld_x[slot], 8, 8 - 8 * slot)
                        if s == 1:
                            pool.wait_ge(bo_done, 1)
                        g_.tensor_tensor(xr, xr, bo_sb.unsqueeze(1).broadcast_to([P, QT, D]), ALU.add).then_inc(x_biased, 1)

            all_steps(pool, step)


def kernel(x, ctx_1024, L0_xattn_W_qkv, L0_xattn_b_qkv, L0_xattn_W_o, L0_xattn_b_o, L0_xattn_ln_gamma,
           L0_xattn_ln_beta):
    import numpy as np
    import concourse.bacc as bacc
    from concourse.bass_utils import run_bass_kernel_spmd

    c = np.ascontiguousarray
    w, b = np.asarray(L0_xattn_W_qkv), np.asarray(L0_xattn_b_qkv)
    xr = np.asarray(x).reshape(B * SQ, D)
    minus = np.zeros((MROWS, HALVES, PACKED), np.float32)
    for f in range(HALVES):
        for h in range(HH):
            minus[f * HH + h, f, h * SKV:(h + 1) * SKV] = -1.0
    cut = LOW_TILES * P
    arrays = {
        "xT": c(xr.T), "x": c(xr), "cT": c(np.asarray(ctx_1024).reshape(B * SKV, D).T),
        "wqT": c(w[:D].T), "wkT": c(w[D:2 * D].T), "wvT": c(w[2 * D:].T), "woT": c(np.asarray(L0_xattn_W_o).T),
        "bias_cols": c(b.reshape(3 * HALVES, P).T),
        "bias_rows": c(np.concatenate([np.asarray(L0_xattn_b_o), np.asarray(L0_xattn_ln_gamma),
                                       np.asarray(L0_xattn_ln_beta)])), "ident": np.eye(P, dtype=np.float32),
        "minus_low": c(minus[:, :, :cut]), "minus_high": c(minus[:, :, cut:]),
    }
    nc = bacc.Bacc("TRN2", target_bir_lowering=False, num_devices=1)
    ins = [nc.dram_tensor(f"in_{k}", list(a.shape), F32, kind="ExternalInput").ap() for k, a in arrays.items()]
    out = nc.dram_tensor("out_dram", [B * SQ, D], F32, kind="ExternalOutput").ap()
    cross_attention_kernel(nc, *ins, out)
    r = run_bass_kernel_spmd(nc, [{f"in_{k}": a for k, a in arrays.items()}], core_ids=[0])
    return r.results[0]["out_dram"].reshape(B, SQ, D)
```
